# Optimizing a Trainium2 kernel written in Bass

```python
import numpy as np
import jax
import jax.numpy as jnp

def _softmax(x, axis=-1):
    return jax.nn.softmax(x, axis=axis)

def _gelu(x):
    return jax.nn.gelu(x, approximate=True)

def _silu(x):
    return jax.nn.silu(x)

def _sigmoid(x):
    return jax.nn.sigmoid(x)

def _layernorm(x, axis=-1, eps=1e-05):
    m = jnp.mean(x, axis=axis, keepdims=True)
    v = jnp.var(x, axis=axis, keepdims=True)
    return (x - m) / jnp.sqrt(v + eps)

def _scatter_add(tgt, idx, src, axis=0):
    return tgt.at[idx].add(src)

def _segment_sum(src, seg, n):
    return jax.ops.segment_sum(src, seg, n)
kernel_name = 'mk_adaln_d1_jaxref_r4_dd0465'

def setup_inputs(seed: int=0):
    np.random.seed(seed)
    _w = jnp.asarray

    def _L0_attn_setup():
        import jax, jax.numpy as jnp
        import numpy as np
        D_MODEL = 256
        NUM_HEADS = 16
        D_HEAD = D_MODEL // NUM_HEADS
        LN_EPS = 1e-05

        def apply_rope(x):
            L = x.shape[2]
            inv_freq = 1.0 / 10000.0 ** (jnp.arange(0, D_HEAD, 2, dtype=jnp.float32) / D_HEAD)
            freqs = jnp.arange(L, dtype=jnp.float32)[:, None] * inv_freq[None, :]
            sin = jnp.sin(freqs)[None, None]
            cos = jnp.cos(freqs)[None, None]
            x1 = x[..., ::2]
            x2 = x[..., 1::2]
            rot = jnp.stack([x1 * cos - x2 * sin, x1 * sin + x2 * cos], axis=-1)
            return rot.reshape(x.shape)
        key = jax.random.key(seed)
        ks = jax.random.split(key, 10)
        B, L = (4, 512)
        s = 1.0 / np.sqrt(D_MODEL)
        inp = {'x': jax.random.normal(ks[0], (B, L, D_MODEL), dtype=jnp.float32), 'ln_gamma': jnp.ones((D_MODEL,), jnp.float32), 'ln_beta': jnp.zeros((D_MODEL,), jnp.float32), 'Wq': jax.random.normal(ks[1], (D_MODEL, D_MODEL), jnp.float32) * s, 'bq': jnp.zeros((D_MODEL,), jnp.float32), 'Wk': jax.random.normal(ks[2], (D_MODEL, D_MODEL), jnp.float32) * s, 'bk': jnp.zeros((D_MODEL,), jnp.float32), 'Wv': jax.random.normal(ks[3], (D_MODEL, D_MODEL), jnp.float32) * s, 'bv': jnp.zeros((D_MODEL,), jnp.float32), 'Wo': jax.random.normal(ks[4], (D_MODEL, D_MODEL), jnp.float32) * s, 'bo': jnp.zeros((D_MODEL,), jnp.float32)}
        return inp
    _L0_attn_in = _L0_attn_setup()

    def _L0_ffn_setup():
        import jax, jax.numpy as jnp
        import numpy as np
        S, B, D, E, C, FF = (512, 4, 256, 8, 512, 1024)
        N = S * B
        key = jax.random.key(seed)
        ks = jax.random.split(key, 7)
        return {'hidden_states': jax.random.normal(ks[0], (S, B, D), dtype=jnp.float32), 'combine_weights': jax.random.uniform(ks[1], (N, E), dtype=jnp.float32), 'top_idx': jax.random.randint(ks[2], (C, E), 0, N, dtype=jnp.int64), 'W1': jax.random.normal(ks[3], (E, D, FF), dtype=jnp.float32) * (1.0 / np.sqrt(D)), 'b1': jnp.zeros((E, FF), dtype=jnp.float32), 'W2': jax.random.normal(ks[4], (E, FF, D), dtype=jnp.float32) * (1.0 / np.sqrt(FF)), 'b2': jnp.zeros((E, D), dtype=jnp.float32)}
    _L0_ffn_in = _L0_ffn_setup()
    _L0_c = _w((lambda *s: np.random.randn(*s).astype(np.float32) * 0.05)(16, 256))
    _L0_wmod = _w((lambda *s: np.random.randn(*s).astype(np.float32) * 0.05)(256, 6 * 256) * 256 ** (-0.5))
    _d = {'L0_attn_x': _L0_attn_in['x'], 'L0_attn_ln_gamma': _L0_attn_in['ln_gamma'], 'L0_attn_ln_beta': _L0_attn_in['ln_beta'], 'L0_attn_Wq': _L0_attn_in['Wq'], 'L0_attn_bq': _L0_attn_in['bq'], 'L0_attn_Wk': _L0_attn_in['Wk'], 'L0_attn_bk': _L0_attn_in['bk'], 'L0_attn_Wv': _L0_attn_in['Wv'], 'L0_attn_bv': _L0_attn_in['bv'], 'L0_attn_Wo': _L0_attn_in['Wo'], 'L0_attn_bo': _L0_attn_in['bo'], 'L0_ffn_combine_weights': _L0_ffn_in['combine_weights'], 'L0_ffn_top_idx': _L0_ffn_in['top_idx'], 'L0_ffn_W1': _L0_ffn_in['W1'], 'L0_ffn_b1': _L0_ffn_in['b1'], 'L0_ffn_W2': _L0_ffn_in['W2'], 'L0_ffn_b2': _L0_ffn_in['b2'], 'L0_c': _L0_c, 'L0_wmod': _L0_wmod}
    _x0 = _d['L0_attn_x']
    _d['L0_attn_x'] = jax.random.normal(jax.random.fold_in(jax.random.key(seed), 1), (16, 1024, 256), dtype=_x0.dtype)
    del _x0
    return _d

def reference(L0_attn_x, L0_attn_ln_gamma, L0_attn_ln_beta, L0_attn_Wq, L0_attn_bq, L0_attn_Wk, L0_attn_bk, L0_attn_Wv, L0_attn_bv, L0_attn_Wo, L0_attn_bo, L0_ffn_combine_weights, L0_ffn_top_idx, L0_ffn_W1, L0_ffn_b1, L0_ffn_W2, L0_ffn_b2, L0_c, L0_wmod):

    def _L0_attn_ref(x, ln_gamma, ln_beta, Wq, bq, Wk, bk, Wv, bv, Wo, bo):
        import jax, jax.numpy as jnp
        import numpy as np
        D_MODEL = 256
        NUM_HEADS = 16
        D_HEAD = D_MODEL // NUM_HEADS
        LN_EPS = 1e-05

        def apply_rope(x):
            L = x.shape[2]
            inv_freq = 1.0 / 10000.0 ** (jnp.arange(0, D_HEAD, 2, dtype=jnp.float32) / D_HEAD)
            freqs = jnp.arange(L, dtype=jnp.float32)[:, None] * inv_freq[None, :]
            sin = jnp.sin(freqs)[None, None]
            cos = jnp.cos(freqs)[None, None]
            x1 = x[..., ::2]
            x2 = x[..., 1::2]
            rot = jnp.stack([x1 * cos - x2 * sin, x1 * sin + x2 * cos], axis=-1)
            return rot.reshape(x.shape)
        B, L, _ = x.shape
        mu = jnp.mean(x, axis=-1, keepdims=True)
        var = jnp.mean(jnp.square(x - mu), axis=-1, keepdims=True)
        xn = (x - mu) * jax.lax.rsqrt(var + LN_EPS) * ln_gamma + ln_beta

        def heads(t):
            return t.reshape(B, L, NUM_HEADS, D_HEAD).transpose(0, 2, 1, 3)
        q = heads(xn @ Wq + bq)
        k = heads(xn @ Wk + bk)
        v = heads(xn @ Wv + bv)
        q = apply_rope(q)
        k = apply_rope(k)
        scores = jnp.einsum('bhid,bhjd->bhij', q, k) / jnp.sqrt(jnp.float32(D_HEAD))
        mask = jnp.tril(jnp.ones((L, L), jnp.float32))[None, None]
        scores = scores * mask + (1.0 - mask) * -1000000000.0
        probs = jax.nn.softmax(scores, axis=-1)
        out = jnp.einsum('bhij,bhjd->bhid', probs, v)
        out = out.transpose(0, 2, 1, 3).reshape(B, L, D_MODEL)
        out = out @ Wo + bo
        return x + out

    def _L0_ffn_ref(hidden_states, combine_weights, top_idx, W1, b1, W2, b2):
        import jax, jax.numpy as jnp
        import numpy as np
        S, B, D, E, C, FF = (512, 4, 256, 8, 512, 1024)
        N = S * B
        s, b, d = hidden_states.shape
        x = hidden_states.reshape(-1, d)
        tok = top_idx.T
        gathered = x[tok]
        h = jax.nn.gelu(jnp.einsum('ecd,edf->ecf', gathered, W1) + b1[:, None, :])
        out_e = jnp.einsum('ecf,efd->ecd', h, W2) + b2[:, None, :]
        e_ids = jnp.arange(tok.shape[0])[:, None]
        w = combine_weights[tok, e_ids]
        weighted = (out_e * w[..., None]).reshape(-1, d)
        out = jnp.zeros_like(x).at[tok.reshape(-1)].add(weighted)
        return out.reshape(s, b, d)
    x = L0_attn_x
    mod = (_silu(L0_c) @ L0_wmod).reshape(L0_c.shape[0], 6, 1, -1)
    sa, ca, ga, sb, cb, gb = (mod[:, 0], mod[:, 1], mod[:, 2], mod[:, 3], mod[:, 4], mod[:, 5])
    ga = (2 * (ga >= 0) - 1) * jnp.maximum(jnp.abs(ga), 0.25)
    gb = (2 * (gb >= 0) - 1) * jnp.maximum(jnp.abs(gb), 0.25)
    h = _layernorm(x, axis=-1) * (1 + ca) + sa
    x = x + ga * _L0_attn_ref(h, L0_attn_ln_gamma, L0_attn_ln_beta, L0_attn_Wq, L0_attn_bq, L0_attn_Wk, L0_attn_bk, L0_attn_Wv, L0_attn_bv, L0_attn_Wo, L0_attn_bo)
    h = _layernorm(x, axis=-1) * (1 + cb) + sb
    x = x + gb * _L0_ffn_ref(h, L0_ffn_combine_weights, L0_ffn_top_idx, L0_ffn_W1, L0_ffn_b1, L0_ffn_W2, L0_ffn_b2)
    return x

_drawn_inputs = setup_inputs


def setup_inputs(seed=0):
    import zlib

    import numpy as np

    out = dict(_drawn_inputs(seed))
    spreads = {'L0_attn_ln_gamma': (1.0, 0.6),
     'L0_attn_ln_beta': (0.0, 0.322),
     'L0_attn_bq': (0.0, 0.8),
     'L0_attn_bk': (0.0, 0.8),
     'L0_attn_bv': (0.0, 0.325),
     'L0_attn_bo': (0.0, 0.341),
     'L0_ffn_b1': (0.0, 0.8),
     'L0_ffn_b2': (0.0, 0.8)}
    factors = {}
    for name, (base, spread) in spreads.items():
        noise = np.random.default_rng([zlib.crc32(name.encode()), seed]).standard_normal(out[name].shape)
        drawn = base * np.exp(spread * noise) if base else spread * noise
        out[name] = jnp.asarray(drawn.astype(out[name].dtype))
    for name, factor in factors.items():
        out[name] = (out[name] * factor).astype(out[name].dtype)
    return out
```

```python
from contextlib import ExitStack

import concourse.bass as bass
import numpy as np
from concourse import mybir

F32 = mybir.dt.float32
BF16 = mybir.dt.bfloat16
I32 = mybir.dt.int32
U32 = mybir.dt.uint32
ALU = mybir.AluOpType
ACT = mybir.ActivationFunctionType
AX = mybir.AxisListType

P = 128
HEADS = 16
NG = 4
HG = HEADS // NG
DMA = 16
EPS = 1e-5
NMOD = 7
M_SA, M_CA1, M_A2, M_GA, M_SB, M_CB1, M_GB = range(NMOD)
Q_TERMS = (0, 1, 2, 0, 1, 0)
K_TERMS = (0, 0, 0, 1, 1, 2)
MASKED = -1.0e30


def wait_apart(eng, sem, value):
    eng.wait_ge(sem, value)
    eng.nop(nofuse=True)


def reuse(eng, sem, value):
    if not isinstance(value, int) or value > 0:
        eng.wait_ge(sem, value)


def split3(eng, link, src, hi, rest, mid, lo):
    link(eng.tensor_copy(hi, src))
    link(eng.tensor_tensor(rest, src, hi, ALU.subtract))
    link(eng.tensor_copy(mid, rest))
    return eng.tensor_tensor(lo, rest, mid, ALU.subtract)


def build(nc, a, out):
    x = a["L0_attn_x"]
    B, L, D = x.shape
    DH = D // HEADS
    T = L // P
    KC = D // P
    ROWS = len(Q_TERMS) * DH
    _, E, = a["L0_ffn_combine_weights"].shape
    SEL = a["L0_ffn_combine_weights"].shape[0]
    C = a["L0_ffn_top_idx"].shape[0]
    FF = a["L0_ffn_W1"].shape[2]
    SB = SEL // L
    assert (DH, KC, ROWS) == (16, 2, 96) and L == 1024 and B % 2 == 0 and SEL == SB * L

    mods_d = nc.dram_tensor("mods", [B, NMOD, D], F32, kind="Internal").ap()
    bias_d = nc.dram_tensor("bias_parts", [3, 3 * D], BF16, kind="Internal").ap()
    out_bias_d = nc.dram_tensor("out_bias_parts", [B, 3, D], BF16, kind="Internal").ap()
    b2_d = nc.dram_tensor("b2_parts", [3, E * D], BF16, kind="Internal").ap()
    resid_d = nc.dram_tensor("resid", [B, P, T, D], F32, kind="Internal").ap()
    q_d = nc.dram_tensor("q_parts", [B, NG, 3, DH * HG, L], BF16, kind="Internal").ap()
    k_d = nc.dram_tensor("k_parts", [B, NG, 3, DH * HG, L], BF16, kind="Internal").ap()
    v_d = nc.dram_tensor("v_ones", [B, NG, P, T * HG * 2 * DH], F32, kind="Internal").ap()
    max_d = nc.dram_tensor("neg_max", [NG, 3, HG * T, P], BF16, kind="Internal").ap()
    att_d = nc.dram_tensor("att", [B, NG, P, L], F32, kind="Internal").ap()
    tok_d = nc.dram_tensor("tok_rows", [SEL, D + E], F32, kind="Internal").ap()

    with ExitStack() as outer:
        keep = lambda n, s, d: outer.enter_context(nc.sbuf_tensor(n, s, d))
        ident = keep("ident", [P, P], F32)
        mask = keep("mask", [P, 512], F32)
        rope = keep("rope", [P, T, 2 * DH], F32)
        w_all = keep("w_all", [P, KC, 3 * D], F32)
        wo = keep("wo", [P, KC, D], F32)
        bias3 = keep("bias3", [3, 3 * D], BF16)
        ones3 = keep("ones3", [3, P], BF16)
        ps = outer.enter_context(nc.psum_tensor("ps", [P, 8, 512], F32))

        phase0(nc, a, ps, ident, mask, rope, w_all, wo, bias3, ones3, mods_d, bias_d, out_bias_d, b2_d, tok_d)
        phase1(nc, x, ps, ident, rope, w_all, bias3, ones3, mods_d, resid_d, q_d, k_d, v_d)
        phase2(nc, B, L, ps, ident, mask, q_d, k_d, v_d, max_d, att_d)
        phase3(nc, B, L, D, ps, ident, wo, ones3, mods_d, out_bias_d, resid_d, att_d, out)
        phase4(nc, a, SB, ps, ident, ones3, mods_d, b2_d, tok_d, out)


def phase0(nc, a, ps, ident, mask, rope, w_all, wo, bias3, ones3, mods_d, bias_d, out_bias_d, b2_d, tok_d):
    B, _, D = mods_d.shape
    KC = D // P
    E = tok_d.shape[1] - D
    T = rope.shape[1]
    scale = (D // HEADS) ** -0.5
    with ExitStack() as ctx:
        sb = lambda n, s, d: ctx.enter_context(nc.sbuf_tensor(n, s, d))
        sem = lambda n: ctx.enter_context(nc.semaphore(n))
        c = sb("c", [B, D], F32)
        e = sb("e", [B, D], F32)
        silu = sb("silu", [B, D], F32)
        silu_t = sb("silu_t", [P, KC, B], F32)
        wmod = sb("wmod", [P, KC, 6 * D], F32)
        w_raw = sb("w_raw", [P, KC, 3 * D], F32)
        gamma = sb("gamma", [P, KC], F32)
        beta = sb("beta", [P, KC], F32)
        brow = sb("brow", [1, 3 * D], F32)
        bo = sb("bo", [B, D], F32)
        mod = sb("mod", [B, 6, D], F32)
        rows = sb("rows", [B, NMOD, D], F32)
        sign = sb("sign", [B, 2, D], F32)
        size = sb("size", [B, 2, D], F32)
        ob = sb("ob", [B, D], F32)
        ob_rest = sb("ob_rest", [B, D], F32)
        ob3 = sb("ob3", [B, 3, D], BF16)
        beff = sb("beff", [1, 3 * D], F32)
        beff_rest = sb("beff_rest", [1, 3 * D], F32)
        beff3 = sb("beff3", [1, 3, 3 * D], BF16)
        b2row = sb("b2row", [1, E * D], F32)
        b2_rest = sb("b2_rest", [1, E * D], F32)
        b2p = sb("b2p", [1, 3, E * D], BF16)
        loaded = sem("p0_loaded")
        comb = sem("p0_comb_copied")
        exp_done = sem("p0_exp_done")
        chain = sem("p0_dve_chain")
        silu_done = sem("p0_silu_done")
        silu_t_done = sem("p0_silu_t_done")
        silu_t_copied = sem("p0_silu_t_copied")
        mod_done = sem("p0_mod_done")
        bias_done = sem("p0_bias_done")
        rows_done = sem("p0_rows_done")
        stored = sem("p0_stored")
        reload = sem("p0_reload")
        block = ctx.enter_context(nc.Block())

        loads = [
            (c[:, :], a["L0_c"]),
            (wmod[:, :, :], a["L0_wmod"].rearrange("(k p) n -> p k n", p=P)),
            (w_raw[:, :, 0:D], a["L0_attn_Wq"].rearrange("(k p) n -> p k n", p=P)),
            (w_raw[:, :, D:2 * D], a["L0_attn_Wk"].rearrange("(k p) n -> p k n", p=P)),
            (w_raw[:, :, 2 * D:3 * D], a["L0_attn_Wv"].rearrange("(k p) n -> p k n", p=P)),
            (wo[:, :, :], a["L0_attn_Wo"].rearrange("(k p) n -> p k n", p=P)),
            (brow[:, 0:D], a["L0_attn_bq"].rearrange("(o n) -> o n", o=1)),
            (brow[:, D:2 * D], a["L0_attn_bk"].rearrange("(o n) -> o n", o=1)),
            (brow[:, 2 * D:3 * D], a["L0_attn_bv"].rearrange("(o n) -> o n", o=1)),
            (bo[:, :], a["L0_attn_bo"].partition_broadcast(B)),
            (b2row[:, :], a["L0_ffn_b2"].rearrange("(o e) d -> o (e d)", o=1)),
            (ident[:, :], a["const_ident"]),
            (mask[:, :], a["const_mask"]),
            (rope[:, :, :], a["const_rope"].rearrange("(t p) n -> p t n", p=P)),
        ]
        small = [
            (gamma[:, :], a["L0_attn_ln_gamma"].rearrange("(k p) -> p k", p=P)),
            (beta[:, :], a["L0_attn_ln_beta"].rearrange("(k p) -> p k", p=P)),
        ]
        LOADED = DMA * (len(loads) + len(small))

        @block.sync
        def _(sp):
            for dst, src in loads:
                sp.dma_start(dst, src).then_inc(loaded, DMA)
            with nc.allow_non_contiguous_dma("one column per contraction chunk"):
                for dst, src in small:
                    sp.dma_start(dst, src).then_inc(loaded, DMA)
                sp.dma_start(tok_d[:, D:D + E], a["L0_ffn_combine_weights"]).then_inc(comb, DMA)
            sp.wait_ge(rows_done, 1)
            sp.dma_start(mods_d, rows[:, :, :]).then_inc(stored, DMA)
            sp.dma_start(out_bias_d, ob3[:, :, :]).then_inc(stored, DMA)
            sp.wait_ge(rows_done, 2)
            sp.dma_start(bias_d.rearrange("(o k) n -> o k n", o=1), beff3[:, :, :]).then_inc(stored, DMA)
            sp.wait_ge(rows_done, 3)
            sp.dma_start(b2_d.rearrange("(o k) n -> o k n", o=1), b2p[:, :, :]).then_inc(stored, DMA)
            sp.wait_ge(stored, 4 * DMA)
            sp.wait_ge(comb, DMA)
            sp.dma_start(bias3[:, :], bias_d).then_inc(reload, DMA)
            sp.wait_ge(reload, DMA)

        @block.scalar
        def _(act):
            act.wait_ge(loaded, LOADED)
            nc.scalar.activation(e[:, :], c[:, :], ACT.Exp, scale=-1.0).then_inc(exp_done, 1)

        @block.tensor
        def _(pe):
            pe.wait_ge(loaded, LOADED)
            pe.wait_ge(silu_done, 1)
            for k in range(KC):
                last = pe.transpose(ps[:, 0, k * B:(k + 1) * B], silu[:, k * P:(k + 1) * P], ident[0:B, 0:B])
            last.then_inc(silu_t_done, 1)
            pe.wait_ge(silu_t_copied, 1)
            for n in range(3):
                for k in range(KC):
                    last = pe.matmul(ps[0:B, 1 + n, :], silu_t[:, k, :], wmod[:, k, n * 512:(n + 1) * 512],
                                     start=(k == 0), stop=(k == KC - 1))
            last.then_inc(mod_done, 1)
            for bank, lo, hi in ((4, 0, 2 * D), (5, 2 * D, 3 * D)):
                for k in range(KC):
                    last = pe.matmul(ps[0:1, bank, 0:hi - lo], beta[:, k:k + 1], w_raw[:, k, lo:hi],
                                     start=(k == 0), stop=(k == KC - 1))
            last.then_inc(bias_done, 1)

        @block.vector
        def _(dve):
            n = [0]

            def link(ins):
                n[0] += 1
                ins.then_inc(chain, 1)
                dve.wait_ge(chain, n[0])

            dve.memset(ones3[:, :], 1.0)
            dve.wait_ge(loaded, LOADED)
            dve.wait_ge(exp_done, 1)
            link(dve.tensor_scalar(e[:, :], e[:, :], 1.0, None, ALU.add))
            link(dve.reciprocal(e[:, :], e[:, :]))
            dve.tensor_tensor(silu[:, :], c[:, :], e[:, :], ALU.mult).then_inc(silu_done, 1)
            for k in range(KC):
                dve.tensor_scalar(w_all[:, k, 0:D], w_raw[:, k, 0:D], gamma[:, k:k + 1], scale, ALU.mult, ALU.mult)
                dve.tensor_scalar(w_all[:, k, D:3 * D], w_raw[:, k, D:3 * D], gamma[:, k:k + 1], None, ALU.mult)
            dve.wait_ge(silu_t_done, 1)
            dve.tensor_copy(silu_t[:, :, :], ps[:, 0, 0:KC * B].rearrange("p (k b) -> p k b", k=KC)) \
               .then_inc(silu_t_copied, 1)
            dve.wait_ge(mod_done, 1)
            link(dve.tensor_copy(mod[:, :, :].rearrange("b m d -> b (m d)"),
                                 ps[0:B, 1:4, :].rearrange("b n d -> b (n d)")))
            gates = mod[:, 2:6:3, :]
            link(dve.tensor_scalar(sign[:, :, :], gates, 0.0, 2.0, ALU.is_ge, ALU.mult))
            link(dve.scalar_tensor_tensor(size[:, :, :], gates, -1.0, gates, ALU.mult, ALU.max))
            link(dve.tensor_scalar(size[:, :, :], size[:, :, :], 0.25, None, ALU.max))
            link(dve.scalar_tensor_tensor(rows[:, M_GA:M_GB + 1:M_GB - M_GA, :], sign[:, :, :], -1.0, size[:, :, :],
                                          ALU.add, ALU.mult))
            link(dve.tensor_copy(rows[:, M_SA, :], mod[:, 0, :]))
            link(dve.tensor_copy(rows[:, M_SB, :], mod[:, 3, :]))
            link(dve.tensor_scalar(rows[:, M_CA1, :], mod[:, 1, :], 1.0, None, ALU.add))
            link(dve.tensor_scalar(rows[:, M_CB1, :], mod[:, 4, :], 1.0, None, ALU.add))
            link(dve.tensor_tensor(rows[:, M_A2, :], rows[:, M_GA, :], rows[:, M_CA1, :], ALU.mult))
            link(dve.tensor_tensor(ob[:, :], mod[:, 0, :], bo[:, :], ALU.add))
            link(dve.tensor_tensor(ob[:, :], ob[:, :], rows[:, M_GA, :], ALU.mult))
            split3(dve, link, ob[:, :], ob3[:, 0, :], ob_rest[:, :], ob3[:, 1, :], ob3[:, 2, :]).then_inc(rows_done, 1)
            dve.wait_ge(bias_done, 1)
            link(dve.tensor_tensor(beff[:, 0:2 * D], ps[0:1, 4, 0:2 * D], brow[:, 0:2 * D], ALU.add))
            link(dve.tensor_tensor(beff[:, 2 * D:3 * D], ps[0:1, 5, 0:D], brow[:, 2 * D:3 * D], ALU.add))
            link(dve.tensor_scalar(beff[:, 0:D], beff[:, 0:D], scale, None, ALU.mult))
            split3(dve, link, beff[:, :], beff3[:, 0, :], beff_rest[:, :], beff3[:, 1, :], beff3[:, 2, :]) \
                .then_inc(rows_done, 1)
            split3(dve, link, b2row[:, :], b2p[:, 0, :], b2_rest[:, :], b2p[:, 1, :], b2p[:, 2, :]) \
                .then_inc(rows_done, 1)


def phase1(nc, x, ps, ident, rope, w_all, bias3, ones3, mods_d, resid_d, q_d, k_d, v_d):
    B, L, D = x.shape
    T = L // P
    KC = D // P
    QK = 2 * D
    NV = HG * 2 * (D // HEADS)
    STORES = 2 * 3 * NG
    PS_X, PS_QK, PS_V, PS_T = 0, 2, 4, 6

    with ExitStack() as ctx:
        sb = lambda n, s, d: ctx.enter_context(nc.sbuf_tensor(n, s, d))
        sem = lambda n: ctx.enter_context(nc.semaphore(n))
        pair = lambda n: (sem(n + "0"), sem(n + "1"))
        xin = sb("xin", [P, 2, T, D], F32)
        mods = sb("mods_b", [P, 2, 3, D], F32)
        h1 = sb("h1", [P, 2, T, D], F32)
        h = sb("h", [P, 2, T, D], F32)
        xn = sb("xn", [P, 2, T, D], F32)
        res = sb("res", [P, 2, T, D], F32)
        st = sb("st", [P, T, 6], F32)
        agx = sb("agx", [P, 2, T, 2], F32)
        agh = sb("agh", [P, 2, T, 2], F32)
        rsx = sb("rsx", [P, 2, T], F32)
        rsh = sb("rsh", [P, 2, T], F32)
        sd = sb("sd", [P, 2, T], F32)
        eps = sb("eps", [P, 1], F32)
        nmx = sb("nmx", [P, 2, T], F32)
        x_t = sb("x_t", [P, 2, KC, P], F32)
        m1 = sb("m1", [P, 2, QK], F32)
        m2 = sb("m2", [P, 2, QK], F32)
        qr = sb("qr", [P, 2, QK], F32)
        rest = sb("rest", [P, 2, QK], F32)
        stage = sb("stage", [P, 2, 3, 4, L], BF16)
        v_st = sb("v_st", [P, 2, NG, T, NV], F32)

        x_in, mod_in = pair("p1_x_in"), pair("p1_mod_in")
        st_done = sem("p1_st")
        agx_done, agh_done = sem("p1_agx"), sem("p1_agh")
        sdx_done, sdh_done = sem("p1_sdx"), sem("p1_sdh")
        rsx_done, rsh_done = sem("p1_rsx"), sem("p1_rsh")
        ones_set = sem("p1_ones_set")
        statx = sem("p1_statx")
        h1_done = sem("p1_h1")
        h_mul = sem("p1_h_mul")
        h_done = sem("p1_h")
        r_mul = sem("p1_r_mul")
        r_done = sem("p1_r")
        xn_done = sem("p1_xn")
        xt_done, xt_copied = sem("p1_xt"), sem("p1_xt_copied")
        qk_done, v_done, v_copied = sem("p1_qk"), sem("p1_v"), sem("p1_v_copied")
        rope_mul, rope_done = sem("p1_rope_mul"), sem("p1_rope")
        qt_done, hi_done, rest_done = sem("p1_qt"), sem("p1_hi"), sem("p1_rest")
        mid_done, lo_done = sem("p1_mid"), sem("p1_lo")
        stage_stored, v_stored, r_stored = pair("p1_stage_stored"), pair("p1_v_stored"), pair("p1_r_stored")
        block = ctx.enter_context(nc.Block())

        def batch(it, n):
            return it * 2 + n, it + n // 2, n % 2

        def run(eng, front, both, back):
            front(batch(0, 0))
            both(batch(0, 1), batch(0, 0))
            both(batch(0, 2), batch(0, 1))
            with eng.Fori(1, B // 2 - 1) as it:
                both(batch(it, 1), batch(it, 0))
                both(batch(it, 2), batch(it, 1))
            last = B // 2 - 1
            both(batch(last, 1), batch(last, 0))
            back(batch(last, 1))

        @block.sync
        def _(sp):
            def front(bt):
                b, half, p = bt
                reuse(sp, r_done, b * T - T)
                reuse(sp, h_done, b * T - T)
                sp.dma_start(xin[:, p], x[b].rearrange("(t p) d -> p t d", p=P)).then_inc(x_in[p], DMA)
                sp.dma_start(mods[:, p], mods_d[b, 0:3, :].partition_broadcast(P)) \
                  .then_inc(mod_in[p], DMA)

            def back(bt):
                b, half, p = bt
                sp.wait_ge(r_done, b * T + T)
                sp.dma_start(resid_d[b], res[:, p]).then_inc(r_stored[p], DMA)
                sp.wait_ge(v_copied, b * T + T)
                for g in range(NG):
                    sp.dma_start(v_d[b, g], v_st[:, p, g].rearrange("p t n -> p (t n)")).then_inc(v_stored[p], DMA)
                sp.wait_ge(mid_done, b * T + T)
                sp.wait_ge(lo_done, b * T + T)
                for which, dst in enumerate((q_d, k_d)):
                    for g in range(NG):
                        for part in range(3):
                            sp.dma_start(dst[b, g, part],
                                         stage[64 * (g % 2):64 * (g % 2) + 64, p, part, 2 * which + g // 2, :]) \
                              .then_inc(stage_stored[p], DMA)

            front(batch(0, 0))
            front(batch(0, 1))
            def two(it):
                front(batch(it, 2))
                back(batch(it, 0))
                front(batch(it, 3))
                back(batch(it, 1))

            two(0)
            with sp.Fori(1, B // 2 - 1) as it:
                two(it)
            back(batch(B // 2 - 1, 0))
            back(batch(B // 2 - 1, 1))
            for p in range(2):
                sp.wait_ge(r_stored[p], DMA * (B // 2))
                sp.wait_ge(v_stored[p], DMA * NG * (B // 2))
                sp.wait_ge(stage_stored[p], DMA * STORES * (B // 2))

        @block.vector
        def _(dve):
            def stats(src, ag, n):
                for t in range(T):
                    ins = dve.bn_stats(st[:, t, :], src[:, t, :])
                ins.then_inc(st_done, 1)
                wait_apart(dve, st_done, n + 1)
                for t in range(T):
                    ins = dve.bn_aggr(ag[:, t, :], st[:, t, :])
                return ins

            def front_x(bt):
                b, half, p = bt
                dve.wait_ge(x_in[p], half * DMA + DMA)
                stats(xin[:, p], agx[:, p], b * 2).then_inc(agx_done, 1)
                dve.wait_ge(sdx_done, b + 1)
                dve.reciprocal(rsx[:, p, :], sd[:, 0, :]).then_inc(rsx_done, 1)
                dve.wait_ge(rsx_done, b + 1)
                dve.scalar_tensor_tensor(nmx[:, p, :], agx[:, p, :, 0], -1.0, rsx[:, p, :], ALU.mult, ALU.mult) \
                   .then_inc(statx, 1)

            def front_h(bt):
                b, half, p = bt
                dve.wait_ge(h_done, b * T + T)
                stats(h[:, p], agh[:, p], b * 2 + 1).then_inc(agh_done, 1)

            def front_xn(bt):
                b, half, p = bt
                dve.wait_ge(sdh_done, b + 1)
                dve.reciprocal(rsh[:, p, :], sd[:, 1, :]).then_inc(rsh_done, 1)
                dve.wait_ge(rsh_done, b + 1)
                reuse(dve, xt_done, b * T - T)
                for t in range(T):
                    dve.tensor_scalar(xn[:, p, t, :], h[:, p, t, :], agh[:, p, t, 0:1], rsh[:, p, t:t + 1],
                                      ALU.subtract, ALU.mult).then_inc(xn_done, 1)

            def rotate(bt, t):
                b, half, p = bt
                s = t % 2
                dve.wait_ge(qk_done, b * T + t + 1)
                if t >= 2:
                    dve.wait_ge(rope_done, b * T + t - 1)
                view = lambda y: y.rearrange("p (x i e) -> p x i e", i=8, e=2)
                cs = rope[:, t, :].rearrange("p (s i e) -> p s i e", s=2, e=2)
                tab = lambda s_: cs[:, s_:s_ + 1].to_broadcast([P, 32, 8, 2])
                bank = ps[:, PS_QK + s, :]
                dve.tensor_tensor(view(m1[:, s, :]), view(bank), tab(0), ALU.mult)
                dve.tensor_tensor(view(m2[:, s, :]), view(bank), tab(1), ALU.mult).then_inc(rope_mul, 1)
                dve.wait_ge(rope_mul, b * T + t + 1)
                reuse(dve, qt_done, b * T + max(t - 1, 0))
                src = lambda y: y[:, s, :].rearrange("p (a h i e) -> p a h i e", a=8, h=HG, e=2)
                dst = qr[:, s, :].rearrange("p (a i e h) -> p a h i e", a=8, h=HG, e=2)
                for e in range(2):
                    ins = dve.tensor_tensor(dst[:, :, :, :, e], src(m1)[:, :, :, :, e], src(m2)[:, :, :, :, 1 - e],
                                            ALU.add)
                ins.then_inc(rope_done, 1)

            def take_rest(bt, t):
                b, half, p = bt
                s = t % 2
                dve.wait_ge(hi_done, b * T + t + 1)
                reuse(dve, lo_done, b * T + max(t - 1, 0))
                dve.tensor_tensor(rest[:, s, :].rearrange("p (a n) -> p a n", a=4),
                                  ps[:, PS_T + s, :].rearrange("p (a n) -> p a n", a=4),
                                  stage[:, p, 0, :, t * P:(t + 1) * P], ALU.subtract).then_inc(rest_done, 1)

            def both(fr, bk):
                if fr is not None:
                    front_x(fr)
                for t in range(T + 1):
                    if t < T:
                        rotate(bk, t)
                    if t >= 1:
                        take_rest(bk, t - 1)
                    if t == 5 and fr is not None:
                        front_h(fr)
                    if t == 6 and fr is not None:
                        front_xn(fr)

            def front(fr):
                front_x(fr)
                front_h(fr)
                front_xn(fr)

            run(dve, front, both, lambda bk: both(None, bk))

        @block.scalar
        def _(act):
            def root(bt, which, ag, ready, done):
                b, half, p = bt
                act.wait_ge(ready, b + 1)
                nc.scalar.activation(sd[:, which, :], ag[:, p, :, 1], ACT.Sqrt, bias=eps[:, :]).then_inc(done, 1)

            def front(bt, tiles):
                b, half, p = bt
                if 0 in tiles:
                    root(bt, 0, agx, agx_done, sdx_done)
                    act.wait_ge(statx, b + 1)
                    reuse(act, r_mul, b * T - T)
                for t in tiles:
                    nc.scalar.activation(h1[:, p, t, :], xin[:, p, t, :], ACT.Identity, bias=nmx[:, p, t:t + 1],
                                         scale=rsx[:, p, t:t + 1]).then_inc(h1_done, 1)

            def copy_x(bt, t):
                b, half, p = bt
                act.wait_ge(xt_done, b * T + t + 1)
                reuse(act, v_done, b * T + max(t - 1, 0))
                nc.scalar.copy(x_t[:, t % 2], ps[:, PS_X + t % 2, 0:D].rearrange("p (k n) -> p k n", k=KC)) \
                  .then_inc(xt_copied, 1)

            def copy_v(bt, t):
                b, half, p = bt
                act.wait_ge(v_done, b * T + t + 1)
                if t == 0:
                    reuse(act, v_stored[p], half * (DMA * NG))
                dst = v_st[:, p, :, t, :].rearrange("p g (h n) -> p g h n", h=HG)[:, :, :, 0:D // HEADS]
                nc.scalar.copy(dst, ps[:, PS_V + t % 2, 0:D].rearrange("p (g h n) -> p g h n", g=NG, h=HG)) \
                  .then_inc(v_copied, 1)

            def high(bt, t):
                b, half, p = bt
                act.wait_ge(qt_done, b * T + t + 1)
                if t == 0:
                    reuse(act, stage_stored[p], half * (DMA * STORES))
                nc.scalar.copy(stage[:, p, 0, :, t * P:(t + 1) * P],
                               ps[:, PS_T + t % 2, :].rearrange("p (a n) -> p a n", a=4)).then_inc(hi_done, 1)

            def middle(bt, t):
                b, half, p = bt
                act.wait_ge(rest_done, b * T + t + 1)
                nc.scalar.copy(stage[:, p, 1, :, t * P:(t + 1) * P],
                               rest[:, t % 2, :].rearrange("p (a n) -> p a n", a=4)).then_inc(mid_done, 1)

            def both(fr, bk):
                copy_x(bk, 0)
                for t in range(T + 2):
                    if t + 1 < T:
                        copy_x(bk, t + 1)
                    if t < T:
                        copy_v(bk, t)
                    if fr is not None and t == 6:
                        root(fr, 1, agh, agh_done, sdh_done)
                    if fr is not None and t < 4:
                        front(fr, range(2 * t, 2 * t + 2))
                    if 1 <= t <= T:
                        high(bk, t - 1)
                    if t >= 2:
                        middle(bk, t - 2)

            act.wait_ge(ones_set, 1)

            def alone(fr):
                front(fr, range(T))
                root(fr, 1, agh, agh_done, sdh_done)

            run(act, alone, both, lambda bk: both(None, bk))

        @block.gpsimd
        def _(pool):
            def scaled(bt, t):
                b, half, p = bt
                if t == 0:
                    pool.wait_ge(mod_in[p], half * DMA + DMA)
                    reuse(pool, xn_done, b * T - T)
                pool.wait_ge(h1_done, b * T + t + 1)
                pool.tensor_tensor(h[:, p, t, :], h1[:, p, t, :], mods[:, p, M_CA1, :], ALU.mult).then_inc(h_mul, 1)
                pool.wait_ge(h_mul, b * T + t + 1)
                pool.tensor_tensor(h[:, p, t, :], h[:, p, t, :], mods[:, p, M_SA, :], ALU.add).then_inc(h_done, 1)

            def residual(bt, t):
                b, half, p = bt
                if t == 0:
                    reuse(pool, r_stored[p], half * DMA)
                pool.tensor_tensor(res[:, p, t, :], h1[:, p, t, :], mods[:, p, M_A2, :], ALU.mult).then_inc(r_mul, 1)
                pool.wait_ge(r_mul, b * T + t + 1)
                pool.tensor_tensor(res[:, p, t, :], res[:, p, t, :], xin[:, p, t, :], ALU.add).then_inc(r_done, 1)

            def low(bt, t):
                b, half, p = bt
                pool.wait_ge(mid_done, b * T + t + 1)
                pool.tensor_tensor(stage[:, p, 2, :, t * P:(t + 1) * P],
                                   rest[:, t % 2, :].rearrange("p (a n) -> p a n", a=4),
                                   stage[:, p, 1, :, t * P:(t + 1) * P], ALU.subtract).then_inc(lo_done, 1)

            def front(fr):
                for t in range(T):
                    scaled(fr, t)
                for t in range(T):
                    residual(fr, t)

            def both(fr, bk):
                for t in range(T):
                    if fr is not None:
                        for u in (2 * (t % 4), 2 * (t % 4) + 1):
                            (scaled if t < 4 else residual)(fr, u)
                    low(bk, t)

            pool.memset(eps[:, :], EPS)
            pool.memset(v_st[:, :, :, :, :], 1.0).then_inc(ones_set, 1)
            run(pool, front, both, lambda bk: both(None, bk))

        @block.tensor
        def _(pe):
            def turn_x(bt, t):
                b, half, p = bt
                pe.wait_ge(xn_done, b * T + t + 1)
                reuse(pe, xt_copied, b * T + max(t - 1, 0))
                for k in range(KC):
                    ins = pe.transpose(ps[:, PS_X + t % 2, k * P:(k + 1) * P], xn[:, p, t, k * P:(k + 1) * P], ident[:, :])
                ins.then_inc(xt_done, 1)

            def project(bt, t):
                b, half, p = bt
                pe.wait_ge(xt_copied, b * T + t + 1)
                reuse(pe, rope_mul, b * T + max(t - 1, 0))
                for bank, lo, hi, done in ((PS_QK + t % 2, 0, QK, qk_done), (PS_V + t % 2, QK, 3 * D, v_done)):
                    if bank >= PS_V:
                        reuse(pe, v_copied, b * T + max(t - 1, 0))
                    o = ps[:, bank, 0:hi - lo]
                    pe.matmul(o, ones3[:, :], bias3[:, lo:hi], start=True, stop=False)
                    for k in range(KC):
                        ins = pe.matmul(o, x_t[:, t % 2, k, :], w_all[:, k, lo:hi], start=False, stop=(k == KC - 1))
                    ins.then_inc(done, 1)

            def turn_qk(bt, t):
                b, half, p = bt
                pe.wait_ge(rope_done, b * T + t + 1)
                reuse(pe, rest_done, b * T + max(t - 1, 0))
                for j in range(4):
                    ins = pe.transpose(ps[:, PS_T + t % 2, j * P:(j + 1) * P], qr[:, t % 2, j * P:(j + 1) * P], ident[:, :])
                ins.then_inc(qt_done, 1)

            def both(fr, bk):
                turn_x(bk, 0)
                for t in range(T + 1):
                    if t + 1 < T:
                        turn_x(bk, t + 1)
                    if t < T:
                        project(bk, t)
                    if t >= 1:
                        turn_qk(bk, t - 1)

            run(pe, lambda fr: None, both, lambda bk: both(None, bk))


def phase2(nc, B, L, ps, ident, mask, q_d, k_d, v_d, max_d, att_d):
    T = L // P
    DH = q_d.shape[3] // HG
    ROWS = len(Q_TERMS) * DH
    AUG = ROWS + 3
    HALF = L // 2
    PIECES = []
    for c in range(2):
        blocks = [(j, max(j * P, c * HALF), (c + 1) * HALF - max(j * P, c * HALF)) for j in range(4 * (c + 1))]
        for k in range(0, len(blocks), 2):
            (j0, q0, w0), (j1, q1, w1) = blocks[k:k + 2]
            at1 = 512 if w0 + w1 > 512 else w0
            PIECES.append((c, [(j0, 0, q0, w0), (j1, at1, q1, w1)]))
    diag = lambda piece: piece[1][0][0] * P == piece[1][0][2] and piece[1][0][0] >= 4 * piece[0]
    width = lambda piece: piece[1][1][1] + piece[1][1][3]
    NPC = len(PIECES)
    NEXP = NPC * HG
    NSEL = sum(diag(p) for p in PIECES) * HG
    CHUNKS = []
    for h in range(HG):
        for i in range(T):
            if i >= 4:
                CHUNKS.append((h, i, 0, 512))
            CHUNKS.append((h, i, 512 * (i // 4), (i % 4 + 1) * P))
    NCH = len(CHUNKS)
    SLOTS = NCH + 1
    NLD = 9
    PS_B, PS_A, PS_O = 0, 4, 6
    UNITS = NG
    AHEAD = 2
    RING = 3

    with ExitStack() as ctx:
        sb = lambda n, s, d: ctx.enter_context(nc.sbuf_tensor(n, s, d))
        sem = lambda n: ctx.enter_context(nc.semaphore(n))
        many = lambda n, k: [sem(f"{n}{i}") for i in range(k)]
        q = sb("q_rows", [P, UNITS, HG, L], BF16)
        k = sb("k_rows", [P, UNITS, HG, L], BF16)
        v = sb("v_rows", [P, UNITS, T, HG, 2 * DH], F32)
        prob = sb("prob", [P, RING, HG, 2 * 512], F32)
        junk = sb("junk", [P, 2, 512], BF16)
        mx = sb("mx", [P, 2, HG, T], F32)
        mx0 = sb("mx0", [P, HG, 4], F32)
        m_rest = sb("m_rest", [HG * T, P], F32)
        m3 = sb("m3", [HG * T, 2, 3, P], BF16)
        o_sb = sb("o_sb", [P, 2, HALF], F32)

        qk_in, v_in, m_in = many("p2_qk_in", UNITS), many("p2_v_in", UNITS), many("p2_m_in", UNITS)
        ones_set = sem("p2_ones_set")
        a_ready, a_free = sem("p2_a_ready"), sem("p2_a_free")
        max_done = sem("p2_max_done")
        m_chain = sem("p2_m_chain")
        m_parts, m_saved = sem("p2_m_parts"), sem("p2_m_saved")
        b_ready, exp_done, sel_done = sem("p2_b_ready"), sem("p2_exp"), sem("p2_sel")
        pv_done, o_copied = sem("p2_pv"), sem("p2_o_copied")
        o_stored = many("p2_o_stored", 2)
        block = ctx.enter_context(nc.Block())

        LAST = B - 1

        def unit(b, n):
            return b + n // NG, n % NG, b * NG + n

        def steps(eng, prologue, step, epilogue=lambda: None):
            prologue()
            for n in range(NG):
                step(unit(0, n), unit(0, n + AHEAD))
            with eng.Fori(1, LAST) as b:
                for n in range(NG):
                    step(unit(b, n), unit(b, n + AHEAD))
            for n in range(NG):
                step(unit(LAST, n), unit(LAST, n + AHEAD) if n + AHEAD < NG else None)
            epilogue()

        @block.sync
        def _(sp):
            def load(un):
                b, g, u = un
                row = lambda d, part, n: d[b, g, part:part + n].rearrange("s (d h) t -> (s d) h t", h=HG)
                for dst, src in (
                    (q[0:48, g], row(q_d, 0, 3)), (q[48:80, g], row(q_d, 0, 2)), (q[80:96, g], row(q_d, 0, 1)),
                    (k[0:16, g], row(k_d, 0, 1)), (k[16:32, g], row(k_d, 0, 1)), (k[32:48, g], row(k_d, 0, 1)),
                    (k[48:64, g], row(k_d, 1, 1)), (k[64:80, g], row(k_d, 1, 1)), (k[80:96, g], row(k_d, 2, 1)),
                ):
                    sp.dma_start(dst, src).then_inc(qk_in[g], DMA)
                sp.dma_start(v[:, g].rearrange("p t h n -> p (t h n)"), v_d[b, g]).then_inc(v_in[g], DMA)

            def maxima(un):
                b, g, u = un
                sp.wait_ge(m_parts, u + 1)
                sp.dma_start(max_d[g].rearrange("s r n -> r s n"), m3[:, g % 2]).then_inc(m_saved, DMA)
                sp.wait_ge(m_saved, u * DMA + DMA)
                sp.dma_start(q[ROWS:AUG, g].rearrange("s h t -> s (h t)"), max_d[g].rearrange("s r n -> s (r n)")) \
                  .then_inc(m_in[g], DMA)

            def prologue():
                for n in range(UNITS):
                    load(unit(0, n))
                maxima(unit(0, 0))
                maxima(unit(0, 1))

            def step(un, ahead):
                b, g, u = un
                if ahead is not None:
                    maxima(ahead)
                if not (isinstance(b, int) and b == LAST):
                    sp.wait_ge(pv_done, u * NPC + NPC)
                    load(unit(b, g + NG))

            steps(sp, prologue, step)

        @block.gpsimd
        def _(pool):
            def step(un, ahead):
                b, g, u = un
                n = 0
                for i, piece in enumerate(PIECES):
                    if not diag(piece):
                        continue
                    for h in range(HG):
                        wait_apart(pool, exp_done, u * NEXP + i * HG + h + 1)
                        at1 = piece[1][1][1]
                        base = prob[:, (g * NPC + i) % RING, h, 0:2 * at1] \
                            .rearrange("p (s n) -> p s n", s=2)[:, :, 0:P]
                        pool.affine_select(out=base, in_=base, compare_op=ALU.is_ge, fill=0.0, base=0,
                                           pattern=[[0, 2], [1, P]], channel_multiplier=-1).then_inc(sel_done, 1)

            steps(pool, lambda: None, step)

        @block.vector
        def _(dve):
            def chunk(un, c):
                b, g, u = un
                h, i, k0, w = CHUNKS[c]
                slot = (g * SLOTS + c) % 2
                wait_apart(dve, a_ready, u * SLOTS + c + 1)
                src = ps[:, PS_A + slot, 0:w]
                if i >= 4 and k0 == 0:
                    ins = dve.tensor_reduce(mx0[:, h, i - 4:i - 3], src, AX.X, ALU.max)
                else:
                    ins = dve.tensor_tensor_reduce(junk[:, slot, 0:w], src, mask[:, 512 - w:512], 1.0, MASKED,
                                                   ALU.add, ALU.max, mx[:, g % 2, h, i:i + 1])
                ins.then_inc(a_free, 1)

            def finish(un):
                b, g, u = un
                dve.wait_ge(a_free, u * SLOTS + NCH)
                late = mx[:, g % 2, :, 4:8]
                dve.tensor_tensor(late, late, mx0[:, :, :], ALU.max).then_inc(max_done, 1)

            def negate(un):
                b, g, u = un
                dve.wait_ge(a_ready, u * SLOTS + SLOTS)
                src = ps[0:HG * T, PS_A + (g * SLOTS + NCH) % 2, 0:P]
                reuse(dve, m_saved, u * DMA - DMA)
                dve.tensor_scalar(m3[:, g % 2, 0, :], src, -1.0, None, ALU.mult).then_inc(m_chain, 1)
                dve.wait_ge(m_chain, u * 2 + 1)
                dve.scalar_tensor_tensor(m_rest[:, :], src, -1.0, m3[:, g % 2, 0, :], ALU.mult, ALU.subtract) \
                   .then_inc(a_free, 1)
                dve.wait_ge(a_free, u * SLOTS + SLOTS)
                dve.tensor_copy(m3[:, g % 2, 1, :], m_rest[:, :]).then_inc(m_chain, 1)
                dve.wait_ge(m_chain, u * 2 + 2)
                dve.tensor_tensor(m3[:, g % 2, 2, :], m_rest[:, :], m3[:, g % 2, 1, :], ALU.subtract) \
                   .then_inc(m_parts, 1)

            def whole(un):
                for c in range(NCH):
                    chunk(un, c)
                finish(un)
                negate(un)

            def prologue():
                dve.memset(k[ROWS:P, :, :, :], 1.0).then_inc(ones_set, 1)
                for n in range(AHEAD):
                    whole(unit(0, n))

            steps(dve, prologue, lambda un, ahead: whole(ahead) if ahead is not None else None)

        @block.scalar
        def _(act):
            def copy_out(un, c):
                b, g, u = un
                act.wait_ge(pv_done, u * NPC + (2 if c == 0 else NPC))
                reuse(act, o_stored[c], u * DMA)
                nc.scalar.copy(o_sb[:, c, :], ps[:, PS_O + c, :]).then_inc(o_copied, 1)
                act.wait_ge(o_copied, u * 2 + c + 1)
                act.dma_start(att_d[b, g, :, c * HALF:(c + 1) * HALF], o_sb[:, c, :]).then_inc(o_stored[c], DMA)

            def exp(un, i):
                b, g, u = un
                w = width(PIECES[i])
                for h in range(HG):
                    n = i * HG + h
                    act.wait_ge(b_ready, u * NEXP + n + 1)
                    if h == 0:
                        reuse(act, pv_done, u * NPC + i + 1 - RING)
                    src = ps[:, PS_B + 2 * (n % 2):PS_B + 2 * (n % 2) + 2, :].rearrange("p s n -> p (s n)")[:, 0:w]
                    nc.scalar.activation(prob[:, (g * NPC + i) % RING, h, 0:w], src, ACT.Exp).then_inc(exp_done, 1)

            def step(un, ahead, first=False):
                b, g, u = un
                for i in range(NPC):
                    exp(un, i)
                    if i == 0 and not first:
                        copy_out(unit(b, g - 1) if g else (b - 1, NG - 1, u - 1), 1)
                    if i == 2:
                        copy_out(un, 0)

            for n in range(NG):
                step(unit(0, n), None, first=(n == 0))
            with act.Fori(1, B) as b:
                for n in range(NG):
                    step(unit(b, n), None)
            copy_out(unit(LAST, NG - 1), 1)
            for c in range(2):
                act.wait_ge(o_stored[c], B * NG * DMA)

        @block.tensor
        def _(pe):
            def scores_for_max(un, c):
                b, g, u = un
                h, i, k0, w = CHUNKS[c]
                if c == 0:
                    pe.wait_ge(qk_in[g], b * (DMA * NLD) + DMA * NLD)
                reuse(pe, a_free, u * SLOTS + max(c - 1, 0))
                pe.matmul(ps[:, PS_A + (g * SLOTS + c) % 2, 0:w], q[0:ROWS, g, h, i * P:(i + 1) * P],
                          k[0:ROWS, g, h, k0:k0 + w], start=True, stop=True).then_inc(a_ready, 1)

            def turn_max(un):
                b, g, u = un
                pe.wait_ge(max_done, u + 1)
                pe.transpose(ps[0:HG * T, PS_A + (g * SLOTS + NCH) % 2, 0:P],
                             mx[:, g % 2].rearrange("p h t -> p (h t)"), ident[:, :]).then_inc(a_ready, 1)

            def scores_for_exp(un, i, h):
                b, g, u = un
                n = i * HG + h
                if n == 0:
                    pe.wait_ge(m_in[g], b * DMA + DMA)
                reuse(pe, exp_done, u * NEXP + max(n - 1, 0))
                for s, (j, at, q0, w) in enumerate(PIECES[i][1]):
                    bank, col = PS_B + 2 * (n % 2) + at // 512, at % 512
                    ins = pe.matmul(ps[:, bank, col:col + w], k[0:AUG, g, h, j * P:(j + 1) * P],
                                    q[0:AUG, g, h, q0:q0 + w], start=True, stop=True)
                ins.then_inc(b_ready, 1)

            def weigh(un, i):
                b, g, u = un
                c, blocks = PIECES[i]
                if i == 0:
                    pe.wait_ge(v_in[g], b * DMA + DMA)
                if i == 0:
                    reuse(pe, o_copied, u * 2 - 1)
                if i == 2:
                    reuse(pe, o_copied, u * 2)
                pe.wait_ge(exp_done, u * NEXP + (i + 1) * HG)
                if diag(PIECES[i]):
                    pe.wait_ge(sel_done, u * NSEL + HG * (1 + sum(diag(x) for x in PIECES[:i])))
                for s, (j, at, q0, w) in enumerate(blocks):
                    for h in range(HG):
                        col = q0 - c * HALF
                        ins = pe.matmul(ps[32 * h:32 * h + 32, PS_O + c, col:col + w], v[:, g, j, h, :],
                                        prob[:, (g * NPC + i) % RING, h, at:at + w],
                                        start=(j == 0), stop=(j == 4 * c + 3), skip_group_check=True)
                ins.then_inc(pv_done, 1)

            def prologue():
                pe.wait_ge(ones_set, 1)
                for n in range(AHEAD):
                    for c in range(NCH):
                        scores_for_max(unit(0, n), c)
                    turn_max(unit(0, n))

            PER = NCH // NEXP
            TURN = 2

            def step(un, ahead, first=False):
                b, g, u = un
                for n in range(NEXP):
                    i, h = n // HG, n % HG
                    scores_for_exp(un, i, h)
                    if ahead is not None:
                        for c in range(n * PER, (n + 1) * PER):
                            scores_for_max(ahead, c)
                    if h == 1 and i >= 1:
                        weigh(un, i - 1)
                if ahead is not None:
                    turn_max(ahead)
                weigh(un, NPC - 1)

            prologue()
            for n in range(NG):
                step(unit(0, n), unit(0, n + AHEAD))
            with pe.Fori(1, LAST) as b:
                for n in range(NG):
                    step(unit(b, n), unit(b, n + AHEAD))
            for n in range(NG):
                step(unit(LAST, n), unit(LAST, n + AHEAD) if n + AHEAD < NG else None)


def phase3(nc, B, L, D, ps, ident, wo, ones3, mods_d, out_bias_d, resid_d, att_d, out):
    T = L // P
    KC = D // P
    DH = D // HEADS
    PS_A, PS_T, PS_C = 0, 2, 4
    with ExitStack() as ctx:
        sb = lambda n, s, d: ctx.enter_context(nc.sbuf_tensor(n, s, d))
        sem = lambda n: ctx.enter_context(nc.semaphore(n))
        pair = lambda n: (sem(n + "0"), sem(n + "1"))
        att = sb("att_b", [P, 2, NG, L], F32)
        res = sb("res_b", [P, 2, T, D], F32)
        gate = sb("gate_b", [P, 2, D], F32)
        ob = sb("ob_b", [3, 2, D], BF16)
        wg = sb("wg", [P, 2, KC, D], F32)
        rec = sb("rec", [P, 2, HEADS], F32)
        norm = sb("norm", [P, 2, D], F32)
        n_t = sb("n_t", [P, 2, KC, P], F32)
        x2 = sb("x2", [P, 2, T, D], F32)
        att_in, small_in, res_in = pair("p3_att_in"), pair("p3_small_in"), pair("p3_res_in")
        wg_done = sem("p3_wg")
        at_done, rec_done, norm_done = sem("p3_at"), sem("p3_rec"), sem("p3_norm")
        nt_done, nt_copied = sem("p3_nt"), sem("p3_nt_copied")
        c_done, x2_done = sem("p3_c"), sem("p3_x2")
        stored = pair("p3_stored")
        block = ctx.enter_context(nc.Block())

        def loop(eng, work):
            for p in range(2):
                work(p, 0, p)
            with eng.Fori(1, B // 2) as it:
                for p in range(2):
                    work(it * 2 + p, it, p)

        def load(sp, b, p):
            sp.dma_start(att[:, p], att_d[b].rearrange("g p t -> p g t")).then_inc(att_in[p], DMA)
            sp.dma_start(res[:, p], resid_d[b]).then_inc(res_in[p], DMA)
            sp.dma_start(gate[:, p], mods_d[b, M_GA, :].partition_broadcast(P)).then_inc(small_in[p], DMA)
            sp.dma_start(ob[:, p], out_bias_d[b]).then_inc(small_in[p], DMA)

        @block.sync
        def _(sp):
            def store(b, p):
                sp.wait_ge(x2_done, b * T + T)
                sp.dma_start(out[b].rearrange("(t p) d -> p t d", p=P), x2[:, p]).then_inc(stored[p], DMA)

            load(sp, 0, 0)
            load(sp, 1, 1)
            for p in range(2):
                store(p, p)
                load(sp, p + 2, p)
            with sp.Fori(1, B // 2 - 1) as it:
                for p in range(2):
                    store(it * 2 + p, p)
                    load(sp, it * 2 + p + 2, p)
            for p in range(2):
                store(B - 2 + p, p)
            for p in range(2):
                sp.wait_ge(stored[p], DMA * (B // 2))

        @block.vector
        def _(dve):
            def work(b, half, p):
                dve.wait_ge(small_in[p], half * (2 * DMA) + 2 * DMA)
                reuse(dve, stored[p], half * DMA)
                for k in range(KC):
                    ins = dve.tensor_tensor(wg[:, p, k, :], wo[:, k, :], gate[:, p, :], ALU.mult)
                ins.then_inc(wg_done, 1)
                dve.wait_ge(res_in[p], half * DMA + DMA)
                for t in range(T + 2):
                    if t < T:
                        s = t % 2
                        dve.wait_ge(at_done, b * T + t + 1)
                        heads = ps[:, PS_A + s, :].rearrange("p (h n) -> p h n", h=HEADS)
                        dve.reciprocal(rec[:, s, :].rearrange("p (h o) -> p h o", o=1), heads[:, :, DH:DH + 1]) \
                           .then_inc(rec_done, 1)
                        dve.wait_ge(rec_done, b * T + t + 1)
                        reuse(dve, nt_done, b * T + max(t - 1, 0))
                        dve.tensor_tensor(norm[:, s, :].rearrange("p (h n) -> p h n", h=HEADS), heads[:, :, 0:DH],
                                          rec[:, s, :].rearrange("p (h o) -> p h o", o=1).to_broadcast([P, HEADS, DH]),
                                          ALU.mult).then_inc(norm_done, 1)
                    if t >= 2:
                        s = t % 2
                        dve.wait_ge(c_done, b * T + t - 1)
                        dve.tensor_tensor(x2[:, p, t - 2, :], ps[:, PS_C + s, 0:D], res[:, p, t - 2, :], ALU.add) \
                           .then_inc(x2_done, 1)

            loop(dve, work)

        @block.scalar
        def _(act):
            def work(b, half, p):
                for t in range(T):
                    act.wait_ge(nt_done, b * T + t + 1)
                    reuse(act, c_done, b * T + max(t - 1, 0))
                    nc.scalar.copy(n_t[:, t % 2], ps[:, PS_T + t % 2, 0:D].rearrange("p (k n) -> p k n", k=KC)) \
                      .then_inc(nt_copied, 1)

            loop(act, work)

        @block.tensor
        def _(pe):
            def work(b, half, p):
                pe.wait_ge(att_in[p], half * DMA + DMA)
                for t in range(T + 2):
                    s = t % 2
                    if t < T:
                        reuse(pe, norm_done, b * T + max(t - 1, 0))
                        for g in range(NG):
                            ins = pe.transpose(ps[:, PS_A + s, g * P:(g + 1) * P], att[:, p, g, t * P:(t + 1) * P],
                                               ident[:, :])
                        ins.then_inc(at_done, 1)
                    if 1 <= t <= T:
                        r = t - 1
                        pe.wait_ge(norm_done, b * T + r + 1)
                        reuse(pe, nt_copied, b * T + max(r - 1, 0))
                        for k in range(KC):
                            ins = pe.transpose(ps[:, PS_T + r % 2, k * P:(k + 1) * P],
                                               norm[:, r % 2, k * P:(k + 1) * P], ident[:, :])
                        ins.then_inc(nt_done, 1)
                    if t >= 2:
                        r = t - 2
                        if r == 0:
                            pe.wait_ge(wg_done, b + 1)
                        pe.wait_ge(nt_copied, b * T + r + 1)
                        reuse(pe, x2_done, b * T + max(r - 1, 0))
                        o = ps[:, PS_C + r % 2, 0:D]
                        pe.matmul(o, ones3[:, :], ob[:, p, :], start=True, stop=False)
                        for k in range(KC):
                            ins = pe.matmul(o, n_t[:, r % 2, k, :], wg[:, p, k, :], start=False, stop=(k == KC - 1))
                        ins.then_inc(c_done, 1)

            loop(pe, work)


def phase4(nc, a, SB, ps, ident, ones3, mods_d, b2_d, tok_d, out):
    SEL, W = tok_d.shape
    D = mods_d.shape[2]
    E = W - D
    C = a["L0_ffn_top_idx"].shape[0]
    FF = a["L0_ffn_W1"].shape[2]
    KC, CT, FT, NT = D // P, C // P, FF // P, SEL // P
    PER_B = NT // SB
    PS_X, PS_H, PS_Y, PS_S = 0, 2, 4, 6
    with ExitStack() as ctx:
        sb = lambda n, s, d: ctx.enter_context(nc.sbuf_tensor(n, s, d))
        sem = lambda n: ctx.enter_context(nc.semaphore(n))
        pair = lambda n: (sem(n + "0"), sem(n + "1"))
        x2 = sb("x2_all", [P, NT, D], F32)
        h2 = sb("h2", [P, NT, D], F32)
        mods = sb("mods_4", [P, SB, 3, D], F32)
        st = sb("st4", [P, NT, 6], F32)
        ag = sb("ag4", [P, NT, 2], F32)
        eps = sb("eps4", [P, 1], F32)
        sd = sb("sd4", [P, NT], F32)
        rs = sb("rs4", [P, NT], F32)
        idx = sb("idx", [P, CT, E], I32)
        idxf = sb("idxf", [P, E, CT], F32)
        iota = sb("iota", [P, SEL], F32)
        b1r = sb("b1r", [E * FT, P], F32)
        b1 = sb("b1", [P, E * FT], F32)
        b2 = sb("b2", [3, E * D], BF16)
        w1 = sb("w1", [P, 2, KC, FF], F32)
        w2 = sb("w2", [P, 2, FT, D], F32)
        gx = sb("gx", [P, 2, CT, W], F32)
        gx_t = sb("gx_t", [P, KC, C], F32)
        hid = sb("hid", [P, FT, C], F32)
        y = sb("y", [P, E * CT, D], F32)
        hot = sb("hot", [P, 2, E * CT, P], F32)
        gated = sb("gated", [P, 2, D], F32)
        x3 = sb("x3", [P, 2, D], F32)

        loaded, x_in = sem("p4_loaded"), sem("p4_x_in")
        w_in = pair("p4_w_in")
        chain = sem("p4_chain")
        ag_done, sd_done, rs_done = sem("p4_ag"), sem("p4_sd"), sem("p4_rs")
        xn_done, h_mul, h_done, h_stored = sem("p4_xn"), sem("p4_h_mul"), sem("p4_h"), sem("p4_h_stored")
        g_in = pair("p4_g_in")
        b1_done, b1_copied = sem("p4_b1"), sem("p4_b1_copied")
        gt_done, gt_copied = sem("p4_gt"), sem("p4_gt_copied")
        hid_done, act_done = sem("p4_hid"), sem("p4_act")
        y_done, y_scaled = sem("p4_y"), sem("p4_y_scaled")
        hot_done, s_done, s_gated, s_added = sem("p4_hot"), sem("p4_s"), sem("p4_s_gated"), sem("p4_s_added")
        stored = pair("p4_stored")
        block = ctx.enter_context(nc.Block())
        NLOAD = 4 + SB

        @block.sync
        def _(sp):
            sp.dma_start(x2[:, :, :], out[0:SB].rearrange("b (t p) d -> p (b t) d", p=P)).then_inc(x_in, DMA)
            for b in range(SB):
                sp.dma_start(mods[:, b], mods_d[b, M_SB:M_GB + 1, :].partition_broadcast(P)) \
                  .then_inc(loaded, DMA)
            with nc.allow_non_contiguous_dma("a few indices per row"):
                sp.dma_start(idx[:, :, :], a["L0_ffn_top_idx"].rearrange("(c p) e -> p c e", p=P)).then_inc(loaded, DMA)
            sp.dma_start(iota[:, :], a["const_iota"].partition_broadcast(P)).then_inc(loaded, DMA)
            sp.dma_start(b1r[:, :], a["L0_ffn_b1"].rearrange("e (f p) -> (e f) p", p=P)).then_inc(loaded, DMA)
            sp.dma_start(b2[:, :], b2_d).then_inc(loaded, DMA)

            def weights(e):
                if e >= 2:
                    sp.wait_ge(y_done, (e - 1) * CT)
                sp.dma_start(w1[:, e % 2], a["L0_ffn_W1"][e].rearrange("(k p) f -> p k f", p=P)).then_inc(w_in[e % 2], DMA)
                sp.dma_start(w2[:, e % 2], a["L0_ffn_W2"][e].rearrange("(f p) d -> p f d", p=P)).then_inc(w_in[e % 2], DMA)

            for e in range(2):
                weights(e)
            sp.wait_ge(h_done, NT)
            sp.dma_start(tok_d[:, 0:D].rearrange("(n p) d -> p n d", p=P), h2[:, :, :]).then_inc(h_stored, DMA)
            for e in range(2, E):
                weights(e)
            for n in range(NT):
                b, t = n // PER_B, n % PER_B
                sp.wait_ge(s_added, n + 1)
                sp.dma_start(out[b, t * P:(t + 1) * P, :], x3[:, n % 2, :]).then_inc(stored[n % 2], DMA)
            for p in range(2):
                sp.wait_ge(stored[p], DMA * (NT // 2))

        @block.gpsimd
        def _(pool):
            pool.wait_ge(loaded, DMA * NLOAD)
            for n in range(NT):
                b = n // PER_B
                pool.wait_ge(xn_done, n + 1)
                pool.tensor_tensor(h2[:, n, :], h2[:, n, :], mods[:, b, 1, :], ALU.mult).then_inc(h_mul, 1)
                pool.wait_ge(h_mul, n + 1)
                pool.tensor_tensor(h2[:, n, :], h2[:, n, :], mods[:, b, 0, :], ALU.add).then_inc(h_done, 1)
            pool.wait_ge(h_stored, DMA)
            for e in range(E):
                if e >= 2:
                    pool.wait_ge(y_scaled, (e - 1) * CT)
                for c in range(CT):
                    pool.indirect_dma_start(
                        gx[:, e % 2, c, :], None, tok_d,
                        bass.IndirectOffsetOnAxis(ap=idx[:, c, e:e + 1].bitcast(U32), axis=0)).then_inc(g_in[e % 2], DMA)

        @block.vector
        def _(dve):
            dve.memset(eps[:, :], EPS)
            dve.wait_ge(x_in, DMA)
            for n in range(NT):
                ins = dve.bn_stats(st[:, n, :], x2[:, n, :])
            ins.then_inc(chain, 1)
            dve.wait_ge(chain, 1)
            for n in range(NT):
                ins = dve.bn_aggr(ag[:, n, :], st[:, n, :])
            ins.then_inc(ag_done, 1)
            dve.wait_ge(sd_done, 1)
            dve.reciprocal(rs[:, :], sd[:, :]).then_inc(rs_done, 1)
            dve.wait_ge(rs_done, 1)
            for n in range(NT):
                dve.tensor_scalar(h2[:, n, :], x2[:, n, :], ag[:, n, 0:1], rs[:, n:n + 1], ALU.subtract, ALU.mult) \
                   .then_inc(xn_done, 1)
            dve.wait_ge(loaded, DMA * NLOAD)
            dve.tensor_copy(idxf[:, :, :], idx[:, :, :].rearrange("p c e -> p e c")).then_inc(chain, 1)
            dve.wait_ge(b1_done, 1)
            dve.tensor_copy(b1[:, :], ps[:, PS_S, 0:E * FT]).then_inc(b1_copied, 1)
            dve.wait_ge(chain, 2)

            def one_hot(n):
                if n >= 2:
                    dve.wait_ge(s_done, n - 1)
                ids = idxf[:, :, :].rearrange("p e (c o) -> p (e c) o", o=1).to_broadcast([P, E * CT, P])
                toks = iota[:, n * P:(n + 1) * P].rearrange("p (o n) -> p o n", o=1).to_broadcast([P, E * CT, P])
                dve.tensor_tensor(hot[:, n % 2], toks, ids, ALU.is_equal).then_inc(hot_done, 1)

            for e in range(E):
                for c in range(CT):
                    dve.wait_ge(gt_done, e * CT + c + 1)
                    if c == 0 and e >= 1:
                        dve.wait_ge(hid_done, e * FT)
                    dve.tensor_copy(gx_t[:, :, c * P:(c + 1) * P],
                                    ps[:, PS_X + c % 2, 0:D].rearrange("p (k n) -> p k n", k=KC)).then_inc(gt_copied, 1)
                for c in range(CT):
                    n = e * CT + c
                    dve.wait_ge(y_done, n + 1)
                    dve.tensor_scalar(y[:, n, :], ps[:, PS_Y + c % 2, 0:D], gx[:, e % 2, c, D + e:D + e + 1], None,
                                      ALU.mult).then_inc(y_scaled, 1)
                if e >= E - 2:
                    one_hot(e - (E - 2))
            for n in range(NT):
                b = n // PER_B
                dve.wait_ge(s_done, n + 1)
                dve.tensor_tensor(gated[:, n % 2, :], ps[:, PS_S + n % 2, 0:D], mods[:, b, 2, :], ALU.mult) \
                   .then_inc(s_gated, 1)
                if n + 2 < NT:
                    one_hot(n + 2)
                dve.wait_ge(s_gated, n + 1)
                if n >= 2:
                    dve.wait_ge(stored[n % 2], DMA * (n // 2))
                dve.tensor_tensor(x3[:, n % 2, :], gated[:, n % 2, :], x2[:, n, :], ALU.add).then_inc(s_added, 1)

        @block.scalar
        def _(act):
            act.wait_ge(ag_done, 1)
            nc.scalar.activation(sd[:, :], ag[:, :, 1], ACT.Sqrt, bias=eps[:, :]).then_inc(sd_done, 1)
            act.wait_ge(b1_copied, 1)
            for e in range(E):
                for f in range(FT):
                    n = e * FT + f
                    act.wait_ge(hid_done, n + 1)
                    if f == 0 and e >= 1:
                        act.wait_ge(y_done, e * CT)
                    nc.scalar.activation(hid[:, f, :], ps[:, PS_H + f % 2, :], ACT.Gelu_apprx_tanh,
                                         bias=b1[:, n:n + 1]).then_inc(act_done, 1)

        @block.tensor
        def _(pe):
            pe.wait_ge(loaded, DMA * NLOAD)
            pe.transpose(ps[:, PS_S, 0:E * FT], b1r[:, :], ident[0:E * FT, 0:E * FT]).then_inc(b1_done, 1)

            def turn(e):
                pe.wait_ge(g_in[e % 2], DMA * CT * (e // 2 + 1))
                for c in range(CT):
                    n = e * CT + c
                    if n >= 2:
                        pe.wait_ge(gt_copied, n - 1)
                    for k in range(KC):
                        ins = pe.transpose(ps[:, PS_X + c % 2, k * P:(k + 1) * P], gx[:, e % 2, c, k * P:(k + 1) * P],
                                           ident[:, :])
                    ins.then_inc(gt_done, 1)

            for e in range(E):
                turn(e)
                pe.wait_ge(w_in[e % 2], 2 * DMA * (e // 2 + 1))
                pe.wait_ge(gt_copied, (e + 1) * CT)
                for f in range(FT):
                    n = e * FT + f
                    if n >= 2:
                        pe.wait_ge(act_done, n - 1)
                    for k in range(KC):
                        ins = pe.matmul(ps[:, PS_H + f % 2, :], w1[:, e % 2, k, f * P:(f + 1) * P], gx_t[:, k, :],
                                        start=(k == 0), stop=(k == KC - 1))
                    ins.then_inc(hid_done, 1)
                pe.wait_ge(act_done, (e + 1) * FT)
                for c in range(CT):
                    n = e * CT + c
                    if n >= 2:
                        pe.wait_ge(y_scaled, n - 1)
                    o = ps[:, PS_Y + c % 2, 0:D]
                    pe.matmul(o, ones3[:, :], b2[:, e * D:(e + 1) * D], start=True, stop=False)
                    for f in range(FT):
                        ins = pe.matmul(o, hid[:, f, c * P:(c + 1) * P], w2[:, e % 2, f, :], start=False,
                                        stop=(f == FT - 1))
                    ins.then_inc(y_done, 1)
            pe.wait_ge(b1_copied, 1)
            pe.wait_ge(y_scaled, E * CT)
            for n in range(NT):
                pe.wait_ge(hot_done, n + 1)
                if n >= 2:
                    pe.wait_ge(s_gated, n - 1)
                for r in range(E * CT):
                    ins = pe.matmul(ps[:, PS_S + n % 2, 0:D], hot[:, n % 2, r, :], y[:, r, :], start=(r == 0),
                                    stop=(r == E * CT - 1))
                ins.then_inc(s_done, 1)


_INS = ['L0_attn_x', 'L0_attn_ln_gamma', 'L0_attn_ln_beta', 'L0_attn_Wq', 'L0_attn_bq', 'L0_attn_Wk', 'L0_attn_bk',
        'L0_attn_Wv', 'L0_attn_bv', 'L0_attn_Wo', 'L0_attn_bo', 'L0_ffn_combine_weights', 'L0_ffn_top_idx',
        'L0_ffn_W1', 'L0_ffn_b1', 'L0_ffn_W2', 'L0_ffn_b2', 'L0_c', 'L0_wmod']


def constants(L, DH, SEL):
    f = np.float32
    rel = np.arange(512)[None, :] - 384 - np.arange(P)[:, None]
    freq = (f(1.0) / f(10000.0) ** (np.arange(0, DH, 2, dtype=f) / f(DH))).astype(f)
    ang = np.arange(L, dtype=f)[:, None] * freq[None, :]
    cos, sin = np.cos(ang).astype(f), np.sin(ang).astype(f)
    table = np.concatenate([np.stack([cos, cos], -1).reshape(L, DH), np.stack([sin, -sin], -1).reshape(L, DH)], 1)
    return {
        "const_ident": np.eye(P, dtype=f),
        "const_mask": np.where(rel > 0, f(MASKED), f(0)).astype(f),
        "const_rope": np.ascontiguousarray(table, dtype=f),
        "const_iota": np.arange(SEL, dtype=f),
    }


def kernel(**inputs):
    import numpy as _np
    import concourse.bacc as _bacc
    from concourse import mybir as _mybir
    from concourse.bass_utils import run_bass_kernel_spmd as _run

    nc = _bacc.Bacc("TRN2", target_bir_lowering=False, num_devices=1)
    arrays, aps = {}, {}
    for name in _INS:
        arrays[name] = _np.ascontiguousarray(inputs[name])
    B, L, D = arrays['L0_attn_x'].shape
    arrays.update(constants(L, D // HEADS, arrays['L0_ffn_combine_weights'].shape[0]))
    for name, arr in arrays.items():
        aps[name] = nc.dram_tensor(f"in_{name}", arr.shape, _mybir.dt.from_np(arr.dtype), kind="ExternalInput").ap()
    out = nc.dram_tensor("out_0", (B, L, D), _mybir.dt.from_np(_np.dtype("float32")), kind="ExternalOutput").ap()
    build(nc, aps, out)
    r = _run(nc, [{f"in_{n}": v for n, v in arrays.items()}], core_ids=[0])
    return r.results[0]["out_0"]
```

```python
from contextlib import ExitStack

import concourse.bass as bass
import numpy as np
from concourse import mybir

F32 = mybir.dt.float32
BF16 = mybir.dt.bfloat16
I32 = mybir.dt.int32
U32 = mybir.dt.uint32
ALU = mybir.AluOpType
ACT = mybir.ActivationFunctionType
AX = mybir.AxisListType

P = 128
HEADS = 16
NG = 4
HG = HEADS // NG
DMA = 16
EPS = 1e-5
NMOD = 7
M_SA, M_CA1, M_A2, M_GA, M_SB, M_CB1, M_GB = range(NMOD)
Q_TERMS = (0, 1, 2, 0, 1, 0)
K_TERMS = (0, 0, 0, 1, 1, 2)
MASKED = -1.0e30


def wait_apart(eng, sem, value):
    eng.wait_ge(sem, value)
    eng.nop(nofuse=True)


def reuse(eng, sem, value):
    if not isinstance(value, int) or value > 0:
        eng.wait_ge(sem, value)


def split3(eng, link, src, hi, rest, mid, lo):
    link(eng.tensor_copy(hi, src))
    link(eng.tensor_tensor(rest, src, hi, ALU.subtract))
    link(eng.tensor_copy(mid, rest))
    return eng.tensor_tensor(lo, rest, mid, ALU.subtract)


def build(nc, a, out):
    x = a["L0_attn_x"]
    B, L, D = x.shape
    DH = D // HEADS
    T = L // P
    KC = D // P
    ROWS = len(Q_TERMS) * DH
    _, E, = a["L0_ffn_combine_weights"].shape
    SEL = a["L0_ffn_combine_weights"].shape[0]
    C = a["L0_ffn_top_idx"].shape[0]
    FF = a["L0_ffn_W1"].shape[2]
    SB = SEL // L
    assert (DH, KC, ROWS) == (16, 2, 96) and L == 1024 and B % 2 == 0 and SEL == SB * L

    mods_d = nc.dram_tensor("mods", [B, NMOD, D], F32, kind="Internal").ap()
    bias_d = nc.dram_tensor("bias_parts", [3, 3 * D], BF16, kind="Internal").ap()
    out_bias_d = nc.dram_tensor("out_bias_parts", [B, 3, D], BF16, kind="Internal").ap()
    b2_d = nc.dram_tensor("b2_parts", [3, E * D], BF16, kind="Internal").ap()
    resid_d = nc.dram_tensor("resid", [B, P, T, D], F32, kind="Internal").ap()
    q_d = nc.dram_tensor("q_parts", [B, NG, 3, DH * HG, L], BF16, kind="Internal").ap()
    k_d = nc.dram_tensor("k_parts", [B, NG, 3, DH * HG, L], BF16, kind="Internal").ap()
    v_d = nc.dram_tensor("v_ones", [B, NG, P, T * HG * 2 * DH], F32, kind="Internal").ap()
    max_d = nc.dram_tensor("neg_max", [NG, 3, HG * T, P], BF16, kind="Internal").ap()
    att_d = nc.dram_tensor("att", [B, NG, P, L], F32, kind="Internal").ap()
    tok_d = nc.dram_tensor("tok_rows", [SEL, D + E], F32, kind="Internal").ap()

    with ExitStack() as outer:
        keep = lambda n, s, d: outer.enter_context(nc.sbuf_tensor(n, s, d))
        ident = keep("ident", [P, P], F32)
        mask = keep("mask", [P, 512], F32)
        rope = keep("rope", [P, T, 2 * DH], F32)
        w_all = keep("w_all", [P, KC, 3 * D], F32)
        wo = keep("wo", [P, KC, D], F32)
        bias3 = keep("bias3", [3, 3 * D], BF16)
        ones3 = keep("ones3", [3, P], BF16)
        ps = outer.enter_context(nc.psum_tensor("ps", [P, 8, 512], F32))

        phase0(nc, a, ps, ident, mask, rope, w_all, wo, bias3, ones3, mods_d, bias_d, out_bias_d, b2_d, tok_d)
        phase1(nc, x, ps, ident, rope, w_all, bias3, ones3, mods_d, resid_d, q_d, k_d, v_d)
        phase2(nc, B, L, ps, ident, mask, q_d, k_d, v_d, max_d, att_d)
        phase3(nc, B, L, D, ps, ident, wo, ones3, mods_d, out_bias_d, resid_d, att_d, out)
        phase4(nc, a, SB, ps, ident, ones3, mods_d, b2_d, tok_d, out)


def phase0(nc, a, ps, ident, mask, rope, w_all, wo, bias3, ones3, mods_d, bias_d, out_bias_d, b2_d, tok_d):
    B, _, D = mods_d.shape
    KC = D // P
    E = tok_d.shape[1] - D
    T = rope.shape[1]
    scale = (D // HEADS) ** -0.5
    with ExitStack() as ctx:
        sb = lambda n, s, d: ctx.enter_context(nc.sbuf_tensor(n, s, d))
        sem = lambda n: ctx.enter_context(nc.semaphore(n))
        c = sb("c", [B, D], F32)
        e = sb("e", [B, D], F32)
        silu = sb("silu", [B, D], F32)
        silu_t = sb("silu_t", [P, KC, B], F32)
        wmod = sb("wmod", [P, KC, 6 * D], F32)
        w_raw = sb("w_raw", [P, KC, 3 * D], F32)
        gamma = sb("gamma", [P, KC], F32)
        beta = sb("beta", [P, KC], F32)
        brow = sb("brow", [1, 3 * D], F32)
        bo = sb("bo", [B, D], F32)
        mod = sb("mod", [B, 6, D], F32)
        rows = sb("rows", [B, NMOD, D], F32)
        sign = sb("sign", [B, 2, D], F32)
        size = sb("size", [B, 2, D], F32)
        ob = sb("ob", [B, D], F32)
        ob_rest = sb("ob_rest", [B, D], F32)
        ob3 = sb("ob3", [B, 3, D], BF16)
        beff = sb("beff", [1, 3 * D], F32)
        beff_rest = sb("beff_rest", [1, 3 * D], F32)
        beff3 = sb("beff3", [1, 3, 3 * D], BF16)
        b2row = sb("b2row", [1, E * D], F32)
        b2_rest = sb("b2_rest", [1, E * D], F32)
        b2p = sb("b2p", [1, 3, E * D], BF16)
        loaded = sem("p0_loaded")
        comb = sem("p0_comb_copied")
        exp_done = sem("p0_exp_done")
        chain = sem("p0_dve_chain")
        silu_done = sem("p0_silu_done")
        silu_t_done = sem("p0_silu_t_done")
        silu_t_copied = sem("p0_silu_t_copied")
        mod_done = sem("p0_mod_done")
        bias_done = sem("p0_bias_done")
        rows_done = sem("p0_rows_done")
        stored = sem("p0_stored")
        reload = sem("p0_reload")
        block = ctx.enter_context(nc.Block())

        loads = [
            (c[:, :], a["L0_c"]),
            (wmod[:, :, :], a["L0_wmod"].rearrange("(k p) n -> p k n", p=P)),
            (w_raw[:, :, 0:D], a["L0_attn_Wq"].rearrange("(k p) n -> p k n", p=P)),
            (w_raw[:, :, D:2 * D], a["L0_attn_Wk"].rearrange("(k p) n -> p k n", p=P)),
            (w_raw[:, :, 2 * D:3 * D], a["L0_attn_Wv"].rearrange("(k p) n -> p k n", p=P)),
            (wo[:, :, :], a["L0_attn_Wo"].rearrange("(k p) n -> p k n", p=P)),
            (brow[:, 0:D], a["L0_attn_bq"].rearrange("(o n) -> o n", o=1)),
            (brow[:, D:2 * D], a["L0_attn_bk"].rearrange("(o n) -> o n", o=1)),
            (brow[:, 2 * D:3 * D], a["L0_attn_bv"].rearrange("(o n) -> o n", o=1)),
            (bo[:, :], a["L0_attn_bo"].partition_broadcast(B)),
            (b2row[:, :], a["L0_ffn_b2"].rearrange("(o e) d -> o (e d)", o=1)),
            (ident[:, :], a["const_ident"]),
            (mask[:, :], a["const_mask"]),
            (rope[:, :, :], a["const_rope"].rearrange("(t p) n -> p t n", p=P)),
        ]
        small = [
            (gamma[:, :], a["L0_attn_ln_gamma"].rearrange("(k p) -> p k", p=P)),
            (beta[:, :], a["L0_attn_ln_beta"].rearrange("(k p) -> p k", p=P)),
        ]
        LOADED = DMA * (len(loads) + len(small))

        @block.sync
        def _(sp):
            for dst, src in loads:
                sp.dma_start(dst, src).then_inc(loaded, DMA)
            with nc.allow_non_contiguous_dma("one column per contraction chunk"):
                for dst, src in small:
                    sp.dma_start(dst, src).then_inc(loaded, DMA)
                sp.dma_start(tok_d[:, D:D + E], a["L0_ffn_combine_weights"]).then_inc(comb, DMA)
            sp.wait_ge(rows_done, 1)
            sp.dma_start(mods_d, rows[:, :, :]).then_inc(stored, DMA)
            sp.dma_start(out_bias_d, ob3[:, :, :]).then_inc(stored, DMA)
            sp.wait_ge(rows_done, 2)
            sp.dma_start(bias_d.rearrange("(o k) n -> o k n", o=1), beff3[:, :, :]).then_inc(stored, DMA)
            sp.wait_ge(rows_done, 3)
            sp.dma_start(b2_d.rearrange("(o k) n -> o k n", o=1), b2p[:, :, :]).then_inc(stored, DMA)
            sp.wait_ge(stored, 4 * DMA)
            sp.wait_ge(comb, DMA)
            sp.dma_start(bias3[:, :], bias_d).then_inc(reload, DMA)
            sp.wait_ge(reload, DMA)

        @block.scalar
        def _(act):
            act.wait_ge(loaded, LOADED)
            nc.scalar.activation(e[:, :], c[:, :], ACT.Exp, scale=-1.0).then_inc(exp_done, 1)

        @block.tensor
        def _(pe):
            pe.wait_ge(loaded, LOADED)
            pe.wait_ge(silu_done, 1)
            for k in range(KC):
                last = pe.transpose(ps[:, 0, k * B:(k + 1) * B], silu[:, k * P:(k + 1) * P], ident[0:B, 0:B])
            last.then_inc(silu_t_done, 1)
            pe.wait_ge(silu_t_copied, 1)
            for n in range(3):
                for k in range(KC):
                    last = pe.matmul(ps[0:B, 1 + n, :], silu_t[:, k, :], wmod[:, k, n * 512:(n + 1) * 512],
                                     start=(k == 0), stop=(k == KC - 1))
            last.then_inc(mod_done, 1)
            for bank, lo, hi in ((4, 0, 2 * D), (5, 2 * D, 3 * D)):
                for k in range(KC):
                    last = pe.matmul(ps[0:1, bank, 0:hi - lo], beta[:, k:k + 1], w_raw[:, k, lo:hi],
                                     start=(k == 0), stop=(k == KC - 1))
            last.then_inc(bias_done, 1)

        @block.vector
        def _(dve):
            n = [0]

            def link(ins):
                n[0] += 1
                ins.then_inc(chain, 1)
                dve.wait_ge(chain, n[0])

            dve.memset(ones3[:, :], 1.0)
            dve.wait_ge(loaded, LOADED)
            dve.wait_ge(exp_done, 1)
            link(dve.tensor_scalar(e[:, :], e[:, :], 1.0, None, ALU.add))
            link(dve.reciprocal(e[:, :], e[:, :]))
            dve.tensor_tensor(silu[:, :], c[:, :], e[:, :], ALU.mult).then_inc(silu_done, 1)
            for k in range(KC):
                dve.tensor_scalar(w_all[:, k, 0:D], w_raw[:, k, 0:D], gamma[:, k:k + 1], scale, ALU.mult, ALU.mult)
                dve.tensor_scalar(w_all[:, k, D:3 * D], w_raw[:, k, D:3 * D], gamma[:, k:k + 1], None, ALU.mult)
            dve.wait_ge(silu_t_done, 1)
            dve.tensor_copy(silu_t[:, :, :], ps[:, 0, 0:KC * B].rearrange("p (k b) -> p k b", k=KC)) \
               .then_inc(silu_t_copied, 1)
            dve.wait_ge(mod_done, 1)
            link(dve.tensor_copy(mod[:, :, :].rearrange("b m d -> b (m d)"),
                                 ps[0:B, 1:4, :].rearrange("b n d -> b (n d)")))
            gates = mod[:, 2:6:3, :]
            link(dve.tensor_scalar(sign[:, :, :], gates, 0.0, 2.0, ALU.is_ge, ALU.mult))
            link(dve.scalar_tensor_tensor(size[:, :, :], gates, -1.0, gates, ALU.mult, ALU.max))
            link(dve.tensor_scalar(size[:, :, :], size[:, :, :], 0.25, None, ALU.max))
            link(dve.scalar_tensor_tensor(rows[:, M_GA:M_GB + 1:M_GB - M_GA, :], sign[:, :, :], -1.0, size[:, :, :],
                                          ALU.add, ALU.mult))
            link(dve.tensor_copy(rows[:, M_SA, :], mod[:, 0, :]))
            link(dve.tensor_copy(rows[:, M_SB, :], mod[:, 3, :]))
            link(dve.tensor_scalar(rows[:, M_CA1, :], mod[:, 1, :], 1.0, None, ALU.add))
            link(dve.tensor_scalar(rows[:, M_CB1, :], mod[:, 4, :], 1.0, None, ALU.add))
            link(dve.tensor_tensor(rows[:, M_A2, :], rows[:, M_GA, :], rows[:, M_CA1, :], ALU.mult))
            link(dve.tensor_tensor(ob[:, :], mod[:, 0, :], bo[:, :], ALU.add))
            link(dve.tensor_tensor(ob[:, :], ob[:, :], rows[:, M_GA, :], ALU.mult))
            split3(dve, link, ob[:, :], ob3[:, 0, :], ob_rest[:, :], ob3[:, 1, :], ob3[:, 2, :]).then_inc(rows_done, 1)
            dve.wait_ge(bias_done, 1)
            link(dve.tensor_tensor(beff[:, 0:2 * D], ps[0:1, 4, 0:2 * D], brow[:, 0:2 * D], ALU.add))
            link(dve.tensor_tensor(beff[:, 2 * D:3 * D], ps[0:1, 5, 0:D], brow[:, 2 * D:3 * D], ALU.add))
            link(dve.tensor_scalar(beff[:, 0:D], beff[:, 0:D], scale, None, ALU.mult))
            split3(dve, link, beff[:, :], beff3[:, 0, :], beff_rest[:, :], beff3[:, 1, :], beff3[:, 2, :]) \
                .then_inc(rows_done, 1)
            split3(dve, link, b2row[:, :], b2p[:, 0, :], b2_rest[:, :], b2p[:, 1, :], b2p[:, 2, :]) \
                .then_inc(rows_done, 1)


def phase1(nc, x, ps, ident, rope, w_all, bias3, ones3, mods_d, resid_d, q_d, k_d, v_d):
    B, L, D = x.shape
    T = L // P
    KC = D // P
    QK = 2 * D
    NV = HG * 2 * (D // HEADS)
    STORES = 2 * 3 * NG
    PS_X, PS_QK, PS_V, PS_T = 0, 2, 4, 6

    with ExitStack() as ctx:
        sb = lambda n, s, d: ctx.enter_context(nc.sbuf_tensor(n, s, d))
        sem = lambda n: ctx.enter_context(nc.semaphore(n))
        pair = lambda n: (sem(n + "0"), sem(n + "1"))
        xin = sb("xin", [P, 2, T, D], F32)
        mods = sb("mods_b", [P, 2, 3, D], F32)
        h1 = sb("h1", [P, 2, T, D], F32)
        h = sb("h", [P, 2, T, D], F32)
        xn = sb("xn", [P, 2, T, D], F32)
        res = sb("res", [P, 2, T, D], F32)
        st = sb("st", [P, T, 6], F32)
        agx = sb("agx", [P, 2, T, 2], F32)
        agh = sb("agh", [P, 2, T, 2], F32)
        rsx = sb("rsx", [P, 2, T], F32)
        rsh = sb("rsh", [P, 2, T], F32)
        sd = sb("sd", [P, 2, T], F32)
        eps = sb("eps", [P, 1], F32)
        nmx = sb("nmx", [P, 2, T], F32)
        x_t = sb("x_t", [P, 2, KC, P], F32)
        m1 = sb("m1", [P, 2, QK], F32)
        m2 = sb("m2", [P, 2, QK], F32)
        qr = sb("qr", [P, 2, QK], F32)
        rest = sb("rest", [P, 2, QK], F32)
        stage = sb("stage", [P, 2, 3, 4, L], BF16)
        v_st = sb("v_st", [P, 2, NG, T, NV], F32)

        x_in, mod_in = pair("p1_x_in"), pair("p1_mod_in")
        st_done = sem("p1_st")
        agx_done, agh_done = sem("p1_agx"), sem("p1_agh")
        sdx_done, sdh_done = sem("p1_sdx"), sem("p1_sdh")
        rsx_done, rsh_done = sem("p1_rsx"), sem("p1_rsh")
        ones_set = sem("p1_ones_set")
        statx = sem("p1_statx")
        h1_done = sem("p1_h1")
        h_mul = sem("p1_h_mul")
        h_done = sem("p1_h")
        r_mul = sem("p1_r_mul")
        r_done = sem("p1_r")
        xn_done = sem("p1_xn")
        xt_done, xt_copied = sem("p1_xt"), sem("p1_xt_copied")
        qk_done, v_done, v_copied = sem("p1_qk"), sem("p1_v"), sem("p1_v_copied")
        rope_mul, rope_done = sem("p1_rope_mul"), sem("p1_rope")
        qt_done, hi_done, rest_done = sem("p1_qt"), sem("p1_hi"), sem("p1_rest")
        mid_done, lo_done = sem("p1_mid"), sem("p1_lo")
        stage_stored, v_stored, r_stored = pair("p1_stage_stored"), pair("p1_v_stored"), pair("p1_r_stored")
        block = ctx.enter_context(nc.Block())

        def batch(it, n):
            return it * 2 + n, it + n // 2, n % 2

        def before(bt):
            b, half, p = bt
            return b - 1, half - (1 - p), 1 - p

        def run(eng, front, both, tail):
            front(batch(0, 0))
            both(batch(0, 1), batch(0, 0), first=True)
            both(batch(0, 2), batch(0, 1))
            with eng.Fori(1, B // 2 - 1) as it:
                both(batch(it, 1), batch(it, 0))
                both(batch(it, 2), batch(it, 1))
            last = B // 2 - 1
            both(batch(last, 1), batch(last, 0))
            both(None, batch(last, 1))
            tail(batch(last, 1))

        @block.sync
        def _(sp):
            def front(bt):
                b, half, p = bt
                reuse(sp, r_done, b * T - T)
                reuse(sp, h_done, b * T - T)
                sp.dma_start(xin[:, p], x[b].rearrange("(t p) d -> p t d", p=P)).then_inc(x_in[p], DMA)
                sp.dma_start(mods[:, p], mods_d[b, 0:3, :].partition_broadcast(P)) \
                  .then_inc(mod_in[p], DMA)

            def back(bt):
                b, half, p = bt
                sp.wait_ge(r_done, b * T + T)
                sp.dma_start(resid_d[b], res[:, p]).then_inc(r_stored[p], DMA)
                sp.wait_ge(v_copied, b * T + T)
                for g in range(NG):
                    sp.dma_start(v_d[b, g], v_st[:, p, g].rearrange("p t n -> p (t n)")).then_inc(v_stored[p], DMA)
                sp.wait_ge(mid_done, b * T + T)
                sp.wait_ge(lo_done, b * T + T)
                for which, dst in enumerate((q_d, k_d)):
                    for g in range(NG):
                        for part in range(3):
                            sp.dma_start(dst[b, g, part],
                                         stage[64 * (g % 2):64 * (g % 2) + 64, p, part, 2 * which + g // 2, :]) \
                              .then_inc(stage_stored[p], DMA)

            front(batch(0, 0))
            front(batch(0, 1))
            def two(it):
                front(batch(it, 2))
                back(batch(it, 0))
                front(batch(it, 3))
                back(batch(it, 1))

            two(0)
            with sp.Fori(1, B // 2 - 1) as it:
                two(it)
            back(batch(B // 2 - 1, 0))
            back(batch(B // 2 - 1, 1))
            for p in range(2):
                sp.wait_ge(r_stored[p], DMA * (B // 2))
                sp.wait_ge(v_stored[p], DMA * NG * (B // 2))
                sp.wait_ge(stage_stored[p], DMA * STORES * (B // 2))

        @block.vector
        def _(dve):
            def stats(src, ag, n):
                for t in range(T):
                    ins = dve.bn_stats(st[:, t, :], src[:, t, :])
                ins.then_inc(st_done, 1)
                wait_apart(dve, st_done, n + 1)
                for t in range(T):
                    ins = dve.bn_aggr(ag[:, t, :], st[:, t, :])
                return ins

            def front_x(bt):
                b, half, p = bt
                dve.wait_ge(x_in[p], half * DMA + DMA)
                stats(xin[:, p], agx[:, p], b * 2).then_inc(agx_done, 1)
                dve.wait_ge(sdx_done, b + 1)
                dve.reciprocal(rsx[:, p, :], sd[:, 0, :]).then_inc(rsx_done, 1)
                dve.wait_ge(rsx_done, b + 1)
                dve.scalar_tensor_tensor(nmx[:, p, :], agx[:, p, :, 0], -1.0, rsx[:, p, :], ALU.mult, ALU.mult) \
                   .then_inc(statx, 1)

            def front_h(bt):
                b, half, p = bt
                dve.wait_ge(h_done, b * T + T)
                stats(h[:, p], agh[:, p], b * 2 + 1).then_inc(agh_done, 1)

            def front_xn(bt):
                b, half, p = bt
                dve.wait_ge(sdh_done, b + 1)
                dve.reciprocal(rsh[:, p, :], sd[:, 1, :]).then_inc(rsh_done, 1)
                dve.wait_ge(rsh_done, b + 1)
                reuse(dve, xt_done, b * T - T)
                for t in range(T):
                    dve.tensor_scalar(xn[:, p, t, :], h[:, p, t, :], agh[:, p, t, 0:1], rsh[:, p, t:t + 1],
                                      ALU.subtract, ALU.mult).then_inc(xn_done, 1)

            def rotate(bt, t):
                b, half, p = bt
                s = t % 2
                dve.wait_ge(qk_done, b * T + t + 1)
                reuse(dve, rope_done, b * T + t - 1)
                view = lambda y: y.rearrange("p (x i e) -> p x i e", i=8, e=2)
                cs = rope[:, t, :].rearrange("p (s i e) -> p s i e", s=2, e=2)
                tab = lambda s_: cs[:, s_:s_ + 1].to_broadcast([P, 32, 8, 2])
                bank = ps[:, PS_QK + s, :]
                dve.tensor_tensor(view(m1[:, s, :]), view(bank), tab(0), ALU.mult)
                dve.tensor_tensor(view(m2[:, s, :]), view(bank), tab(1), ALU.mult).then_inc(rope_mul, 1)
                dve.wait_ge(rope_mul, b * T + t + 1)
                reuse(dve, qt_done, b * T + t - 1)
                src = lambda y: y[:, s, :].rearrange("p (a h i e) -> p a h i e", a=8, h=HG, e=2)
                dst = qr[:, s, :].rearrange("p (a i e h) -> p a h i e", a=8, h=HG, e=2)
                for e in range(2):
                    ins = dve.tensor_tensor(dst[:, :, :, :, e], src(m1)[:, :, :, :, e], src(m2)[:, :, :, :, 1 - e],
                                            ALU.add)
                ins.then_inc(rope_done, 1)

            def take_rest(bt, t):
                b, half, p = bt
                s = t % 2
                dve.wait_ge(hi_done, b * T + t + 1)
                reuse(dve, lo_done, b * T + t - 1)
                dve.tensor_tensor(rest[:, s, :].rearrange("p (a n) -> p a n", a=4),
                                  ps[:, PS_T + s, :].rearrange("p (a n) -> p a n", a=4),
                                  stage[:, p, 0, :, t * P:(t + 1) * P], ALU.subtract).then_inc(rest_done, 1)

            def both(fr, bk, first=False):
                if fr is not None:
                    front_x(fr)
                for t in range(T):
                    rotate(bk, t)
                    if t >= 1:
                        take_rest(bk, t - 1)
                    elif not first:
                        take_rest(before(bk), T - 1)
                    if t == 5 and fr is not None:
                        front_h(fr)
                    if t == 6 and fr is not None:
                        front_xn(fr)

            def front(fr):
                front_x(fr)
                front_h(fr)
                front_xn(fr)

            run(dve, front, both, lambda bk: take_rest(bk, T - 1))

        @block.scalar
        def _(act):
            def root(bt, which, ag, ready, done):
                b, half, p = bt
                act.wait_ge(ready, b + 1)
                nc.scalar.activation(sd[:, which, :], ag[:, p, :, 1], ACT.Sqrt, bias=eps[:, :]).then_inc(done, 1)

            def front(bt, tiles):
                b, half, p = bt
                if 0 in tiles:
                    root(bt, 0, agx, agx_done, sdx_done)
                    act.wait_ge(statx, b + 1)
                    reuse(act, r_mul, b * T - T)
                for t in tiles:
                    nc.scalar.activation(h1[:, p, t, :], xin[:, p, t, :], ACT.Identity, bias=nmx[:, p, t:t + 1],
                                         scale=rsx[:, p, t:t + 1]).then_inc(h1_done, 1)

            def copy_x(bt, t):
                b, half, p = bt
                act.wait_ge(xt_done, b * T + t + 1)
                reuse(act, v_done, b * T + t - 1)
                nc.scalar.copy(x_t[:, t % 2], ps[:, PS_X + t % 2, 0:D].rearrange("p (k n) -> p k n", k=KC)) \
                  .then_inc(xt_copied, 1)

            def copy_v(bt, t):
                b, half, p = bt
                act.wait_ge(v_done, b * T + t + 1)
                if t == 0:
                    reuse(act, v_stored[p], half * (DMA * NG))
                dst = v_st[:, p, :, t, :].rearrange("p g (h n) -> p g h n", h=HG)[:, :, :, 0:D // HEADS]
                nc.scalar.copy(dst, ps[:, PS_V + t % 2, 0:D].rearrange("p (g h n) -> p g h n", g=NG, h=HG)) \
                  .then_inc(v_copied, 1)

            def high(bt, t):
                b, half, p = bt
                act.wait_ge(qt_done, b * T + t + 1)
                if t == 0:
                    reuse(act, stage_stored[p], half * (DMA * STORES))
                nc.scalar.copy(stage[:, p, 0, :, t * P:(t + 1) * P],
                               ps[:, PS_T + t % 2, :].rearrange("p (a n) -> p a n", a=4)).then_inc(hi_done, 1)

            def middle(bt, t):
                b, half, p = bt
                act.wait_ge(rest_done, b * T + t + 1)
                nc.scalar.copy(stage[:, p, 1, :, t * P:(t + 1) * P],
                               rest[:, t % 2, :].rearrange("p (a n) -> p a n", a=4)).then_inc(mid_done, 1)

            def both(fr, bk, first=False):
                if first:
                    copy_x(bk, 0)
                for t in range(T):
                    if t + 1 < T:
                        copy_x(bk, t + 1)
                    elif fr is not None:
                        copy_x(fr, 0)
                    copy_v(bk, t)
                    if fr is not None and t == 6:
                        root(fr, 1, agh, agh_done, sdh_done)
                    if fr is not None and t < 4:
                        front(fr, range(2 * t, 2 * t + 2))
                    if t >= 1:
                        high(bk, t - 1)
                    elif not first:
                        high(before(bk), T - 1)
                    if t >= 2:
                        middle(bk, t - 2)
                    elif not first:
                        middle(before(bk), T + t - 2)

            act.wait_ge(ones_set, 1)

            def alone(fr):
                front(fr, range(T))
                root(fr, 1, agh, agh_done, sdh_done)

            def tail(bk):
                high(bk, T - 1)
                middle(bk, T - 2)
                middle(bk, T - 1)

            run(act, alone, both, tail)

        @block.gpsimd
        def _(pool):
            def scaled(bt, t):
                b, half, p = bt
                if t == 0:
                    pool.wait_ge(mod_in[p], half * DMA + DMA)
                    reuse(pool, xn_done, b * T - T)
                pool.wait_ge(h1_done, b * T + t + 1)
                pool.tensor_tensor(h[:, p, t, :], h1[:, p, t, :], mods[:, p, M_CA1, :], ALU.mult).then_inc(h_mul, 1)
                pool.wait_ge(h_mul, b * T + t + 1)
                pool.tensor_tensor(h[:, p, t, :], h[:, p, t, :], mods[:, p, M_SA, :], ALU.add).then_inc(h_done, 1)

            def residual(bt, t):
                b, half, p = bt
                if t == 0:
                    reuse(pool, r_stored[p], half * DMA)
                pool.tensor_tensor(res[:, p, t, :], h1[:, p, t, :], mods[:, p, M_A2, :], ALU.mult).then_inc(r_mul, 1)
                pool.wait_ge(r_mul, b * T + t + 1)
                pool.tensor_tensor(res[:, p, t, :], res[:, p, t, :], xin[:, p, t, :], ALU.add).then_inc(r_done, 1)

            def low(bt, t):
                b, half, p = bt
                pool.wait_ge(mid_done, b * T + t + 1)
                pool.tensor_tensor(stage[:, p, 2, :, t * P:(t + 1) * P],
                                   rest[:, t % 2, :].rearrange("p (a n) -> p a n", a=4),
                                   stage[:, p, 1, :, t * P:(t + 1) * P], ALU.subtract).then_inc(lo_done, 1)

            def front(fr):
                for t in range(T):
                    scaled(fr, t)
                for t in range(T):
                    residual(fr, t)

            def both(fr, bk, first=False):
                for t in range(T):
                    if t >= 2:
                        low(bk, t - 2)
                    elif not first:
                        low(before(bk), T + t - 2)
                    if fr is not None:
                        for u in (2 * (t % 4), 2 * (t % 4) + 1):
                            (scaled if t < 4 else residual)(fr, u)

            def tail(bk):
                low(bk, T - 2)
                low(bk, T - 1)

            pool.memset(eps[:, :], EPS)
            pool.memset(v_st[:, :, :, :, :], 1.0).then_inc(ones_set, 1)
            run(pool, front, both, tail)

        @block.tensor
        def _(pe):
            def turn_x(bt, t):
                b, half, p = bt
                pe.wait_ge(xn_done, b * T + t + 1)
                reuse(pe, xt_copied, b * T + t - 1)
                for k in range(KC):
                    ins = pe.transpose(ps[:, PS_X + t % 2, k * P:(k + 1) * P], xn[:, p, t, k * P:(k + 1) * P], ident[:, :])
                ins.then_inc(xt_done, 1)

            def project(bt, t):
                b, half, p = bt
                pe.wait_ge(xt_copied, b * T + t + 1)
                reuse(pe, rope_mul, b * T + t - 1)
                for bank, lo, hi, done in ((PS_QK + t % 2, 0, QK, qk_done), (PS_V + t % 2, QK, 3 * D, v_done)):
                    if bank >= PS_V:
                        reuse(pe, v_copied, b * T + t - 1)
                    o = ps[:, bank, 0:hi - lo]
                    pe.matmul(o, ones3[:, :], bias3[:, lo:hi], start=True, stop=False)
                    for k in range(KC):
                        ins = pe.matmul(o, x_t[:, t % 2, k, :], w_all[:, k, lo:hi], start=False, stop=(k == KC - 1))
                    ins.then_inc(done, 1)

            def turn_qk(bt, t):
                b, half, p = bt
                pe.wait_ge(rope_done, b * T + t + 1)
                reuse(pe, rest_done, b * T + t - 1)
                for j in range(4):
                    ins = pe.transpose(ps[:, PS_T + t % 2, j * P:(j + 1) * P], qr[:, t % 2, j * P:(j + 1) * P], ident[:, :])
                ins.then_inc(qt_done, 1)

            def both(fr, bk, first=False):
                if first:
                    turn_x(bk, 0)
                for t in range(T):
                    if t + 1 < T:
                        turn_x(bk, t + 1)
                    elif fr is not None:
                        turn_x(fr, 0)
                    project(bk, t)
                    if t >= 1:
                        turn_qk(bk, t - 1)
                    elif not first:
                        turn_qk(before(bk), T - 1)

            run(pe, lambda fr: None, both, lambda bk: turn_qk(bk, T - 1))


def phase2(nc, B, L, ps, ident, mask, q_d, k_d, v_d, max_d, att_d):
    T = L // P
    DH = q_d.shape[3] // HG
    ROWS = len(Q_TERMS) * DH
    AUG = ROWS + 3
    HALF = L // 2
    PIECES = []
    for c in range(2):
        block = lambda j, at: (j, at, max(j * P, c * HALF), (c + 1) * HALF - max(j * P, c * HALF))
        PIECES += [(c, [block(j, 0)]) for j in range(4 * c + 1)]
        PIECES += [(c, [block(4 * c + 1, 0), block(4 * c + 3, 384)]), (c, [block(4 * c + 2, 0)])]
    diag = lambda piece: piece[1][0][0] >= 4 * piece[0]
    width = lambda piece: sum(w for _, _, _, w in piece[1])
    HALF0 = sum(c == 0 for c, _ in PIECES)
    NPC = len(PIECES)
    NEXP = NPC * HG
    cut = lambda pieces: sum(len(p[1]) for p in pieces if diag(p))
    NSEL = cut(PIECES)
    LAG = 2
    WIDE, NARROW = [], []
    for h in range(HG):
        for i in range(T):
            if i >= 4:
                WIDE.append((h, i, 0, 512))
            w = (i % 4 + 1) * P
            (WIDE if w == 512 else NARROW).append((h, i, 512 * (i // 4), w))
    NCH = len(WIDE) + len(NARROW)
    CHUNKS, WITH = [], []
    for i in range(NPC):
        take = (i + 1) * NCH // NPC - i * NCH // NPC
        for kinds in ("n" * (take - 3), "w", "n", "w"):
            WITH.append(range(len(CHUNKS), len(CHUNKS) + len(kinds)))
            CHUNKS += [(NARROW if kind == "n" and NARROW else WIDE).pop(0) for kind in kinds]
    TURN = 6
    USERS = NCH + 1
    NLD = 9
    PS_B, PS_A, PS_O = 0, 3, 6
    BANKS = 3
    UNITS = NG
    AHEAD = 2
    RING = 5

    with ExitStack() as ctx:
        sb = lambda n, s, d: ctx.enter_context(nc.sbuf_tensor(n, s, d))
        sem = lambda n: ctx.enter_context(nc.semaphore(n))
        many = lambda n, k: [sem(f"{n}{i}") for i in range(k)]
        q = sb("q_rows", [P, UNITS, HG, L], BF16)
        k = sb("k_rows", [P, UNITS, HG, L], BF16)
        v = sb("v_rows", [P, UNITS, T, HG, 2 * DH], F32)
        prob = sb("prob", [P, RING, HG, 512], F32)
        junk = sb("junk", [P, BANKS, 512], BF16)
        mx = sb("mx", [P, 2, HG, T], F32)
        mx0 = sb("mx0", [P, 2, HG, 4], F32)
        m_rest = sb("m_rest", [HG * T, P], F32)
        m3 = sb("m3", [HG * T, 2, 3, P], BF16)
        o_sb = sb("o_sb", [P, 2, HALF], F32)

        qk_in, v_in, m_in = many("p2_qk_in", UNITS), many("p2_v_in", UNITS), many("p2_m_in", UNITS)
        ones_set = sem("p2_ones_set")
        a_ready, a_free = sem("p2_a_ready"), sem("p2_a_free")
        turned, turn_free = sem("p2_turned"), sem("p2_turn_free")
        max_done = sem("p2_max_done")
        m_chain = sem("p2_m_chain")
        m_parts, m_saved = sem("p2_m_parts"), sem("p2_m_saved")
        b_ready, exp_done, sel_done = sem("p2_b_ready"), sem("p2_exp"), sem("p2_sel")
        pv_done, o_copied = sem("p2_pv"), sem("p2_o_copied")
        o_stored = many("p2_o_stored", 2)
        block = ctx.enter_context(nc.Block())

        LAST = B - 1

        def unit(b, n):
            return b + n // NG, n % NG, b * NG + n

        def bank(g, n):
            return (n + g) % BANKS

        def earlier(u, g, n, per):
            return u * per + (n + 1 - BANKS if g or n else 0)

        assert NEXP % BANKS == 1 and USERS % BANKS == 1

        def chunk_bank(g, c):
            return PS_A + bank(g, c + (c >= TURN))

        def steps(eng, prologue, step, epilogue=lambda: None):
            prologue()
            for n in range(NG):
                step(unit(0, n), unit(0, n + AHEAD))
            with eng.Fori(1, LAST) as b:
                for n in range(NG):
                    step(unit(b, n), unit(b, n + AHEAD))
            for n in range(NG):
                step(unit(LAST, n), unit(LAST, n + AHEAD) if n + AHEAD < NG else None)
            epilogue()

        @block.sync
        def _(sp):
            def load(un):
                b, g, u = un
                row = lambda d, part, n: d[b, g, part:part + n].rearrange("s (d h) t -> (s d) h t", h=HG)
                for dst, src in (
                    (q[0:48, g], row(q_d, 0, 3)), (q[48:80, g], row(q_d, 0, 2)), (q[80:96, g], row(q_d, 0, 1)),
                    (k[0:16, g], row(k_d, 0, 1)), (k[16:32, g], row(k_d, 0, 1)), (k[32:48, g], row(k_d, 0, 1)),
                    (k[48:64, g], row(k_d, 1, 1)), (k[64:80, g], row(k_d, 1, 1)), (k[80:96, g], row(k_d, 2, 1)),
                ):
                    sp.dma_start(dst, src).then_inc(qk_in[g], DMA)
                sp.dma_start(v[:, g].rearrange("p t h n -> p (t h n)"), v_d[b, g]).then_inc(v_in[g], DMA)

            def maxima(un):
                b, g, u = un
                sp.wait_ge(m_parts, u + 1)
                sp.dma_start(max_d[g].rearrange("s r n -> r s n"), m3[:, g % 2]).then_inc(m_saved, DMA)
                sp.wait_ge(m_saved, u * DMA + DMA)
                sp.dma_start(q[ROWS:AUG, g].rearrange("s h t -> s (h t)"), max_d[g].rearrange("s r n -> s (r n)")) \
                  .then_inc(m_in[g], DMA)

            def prologue():
                for n in range(UNITS):
                    load(unit(0, n))
                maxima(unit(0, 0))
                maxima(unit(0, 1))

            def step(un, ahead):
                b, g, u = un
                if ahead is not None:
                    maxima(ahead)
                if not (isinstance(b, int) and b == LAST):
                    sp.wait_ge(pv_done, u * NPC + NPC)
                    load(unit(b, g + NG))

            steps(sp, prologue, step)

        @block.gpsimd
        def _(pool):
            def step(un, ahead):
                b, g, u = un
                for i, piece in enumerate(PIECES):
                    if not diag(piece):
                        continue
                    wait_apart(pool, exp_done, u * NEXP + (i + 1) * HG)
                    for _, at, _, _ in piece[1]:
                        own = prob[:, (g * NPC + i) % RING, :, at:at + P]
                        pool.affine_select(out=own, in_=own, compare_op=ALU.is_ge, fill=0.0, base=0,
                                           pattern=[[0, HG], [1, P]], channel_multiplier=-1).then_inc(sel_done, 1)

            def prologue():
                for g in range(NG):
                    pool.memset(k[ROWS:P, g], 1.0).then_inc(ones_set, 1)

            steps(pool, prologue, step)

        @block.vector
        def _(dve):
            def chunk(un, c):
                b, g, u = un
                h, i, k0, w = CHUNKS[c]
                at = chunk_bank(g, c)
                wait_apart(dve, a_ready, u * NCH + c + 1)
                src = ps[:, at, 0:w]
                if i >= 4 and k0 == 0:
                    ins = dve.tensor_reduce(mx0[:, g % 2, h, i - 4:i - 3], src, AX.X, ALU.max)
                else:
                    ins = dve.tensor_tensor_reduce(junk[:, at - PS_A, 0:w], src, mask[:, 512 - w:512], 1.0, MASKED,
                                                   ALU.add, ALU.max, mx[:, g % 2, h, i:i + 1])
                ins.then_inc(a_free, 1)

            def finish(un):
                b, g, u = un
                dve.wait_ge(a_free, u * NCH + NCH)
                late = mx[:, g % 2, :, 4:8]
                dve.tensor_tensor(late, late, mx0[:, g % 2], ALU.max).then_inc(max_done, 1)

            def negate(un, stage):
                b, g, u = un
                src = ps[0:HG * T, PS_A + bank((g + 1) % NG, TURN), 0:P]
                hi, mid, lo = (m3[:, g % 2, s, :] for s in range(3))
                if stage == 0:
                    dve.wait_ge(turned, u + 1)
                    reuse(dve, m_saved, u * DMA - DMA)
                    dve.tensor_scalar(hi, src, -1.0, None, ALU.mult).then_inc(m_chain, 1)
                elif stage == 1:
                    dve.wait_ge(m_chain, u * 2 + 1)
                    dve.scalar_tensor_tensor(m_rest[:, :], src, -1.0, hi, ALU.mult, ALU.subtract) \
                       .then_inc(turn_free, 1)
                elif stage == 2:
                    dve.wait_ge(turn_free, u + 1)
                    dve.tensor_copy(mid, m_rest[:, :]).then_inc(m_chain, 1)
                else:
                    dve.wait_ge(m_chain, u * 2 + 2)
                    dve.tensor_tensor(lo, m_rest[:, :], mid, ALU.subtract).then_inc(m_parts, 1)

            def before(un):
                b, g, u = un
                return (b, g - 1, u - 1) if g else (b - 1, NG - 1, u - 1)

            def whole(un, first=False):
                for c in range(NCH):
                    if c == 2 and not first:
                        finish(before(un))
                    if TURN <= c < TURN + 4 and not first:
                        negate(before(un), c - TURN)
                    chunk(un, c)

            def prologue():
                for n in range(AHEAD):
                    whole(unit(0, n), first=(n == 0))

            def step(un, ahead):
                if ahead is not None:
                    whole(ahead)
                elif un[1] == NG - AHEAD:
                    finish(unit(LAST, NG - 1))
                    for stage in range(4):
                        negate(unit(LAST, NG - 1), stage)

            steps(dve, prologue, step)

        @block.scalar
        def _(act):
            def copy_out(un, c):
                b, g, u = un
                act.wait_ge(pv_done, u * NPC + (HALF0 if c == 0 else NPC))
                reuse(act, o_stored[c], u * DMA)
                nc.scalar.copy(o_sb[:, c, :], ps[:, PS_O + c, :]).then_inc(o_copied, 1)
                act.wait_ge(o_copied, u * 2 + c + 1)
                act.dma_start(att_d[b, g, :, c * HALF:(c + 1) * HALF], o_sb[:, c, :]).then_inc(o_stored[c], DMA)

            def exp(un, i):
                b, g, u = un
                w = width(PIECES[i])
                for h in range(HG):
                    n = i * HG + h
                    act.wait_ge(b_ready, u * NEXP + n + 1)
                    if h == 0:
                        reuse(act, pv_done, u * NPC + i + 1 - RING)
                    src = ps[:, PS_B + bank(g, n), 0:w]
                    nc.scalar.activation(prob[:, (g * NPC + i) % RING, h, 0:w], src, ACT.Exp).then_inc(exp_done, 1)

            def step(un, ahead, first=False):
                b, g, u = un
                for i in range(NPC):
                    exp(un, i)
                    if i == LAG and not first:
                        copy_out((b, g - 1, u - 1) if g else (b - 1, NG - 1, u - 1), 1)
                    if i == HALF0 + LAG:
                        copy_out(un, 0)

            for n in range(NG):
                step(unit(0, n), None, first=(n == 0))
            with act.Fori(1, B) as b:
                for n in range(NG):
                    step(unit(b, n), None)
            copy_out(unit(LAST, NG - 1), 1)
            for c in range(2):
                act.wait_ge(o_stored[c], B * NG * DMA)

        @block.tensor
        def _(pe):
            def scores_for_max(un, c):
                b, g, u = un
                h, i, k0, w = CHUNKS[c]
                if c == 0:
                    pe.wait_ge(qk_in[g], b * (DMA * NLD) + DMA * NLD)
                user = c + (c >= TURN)
                if user - BANKS == TURN:
                    reuse(pe, turn_free, u)
                ahead_of = user - BANKS + 1 - (user - BANKS >= TURN)
                reuse(pe, a_free, u * NCH + (ahead_of if g or c else 0))
                pe.matmul(ps[:, chunk_bank(g, c), 0:w], q[0:ROWS, g, h, i * P:(i + 1) * P],
                          k[0:ROWS, g, h, k0:k0 + w], start=True, stop=True).then_inc(a_ready, 1)

            def turn_max(un, last=False):
                b, g, u = un
                pe.wait_ge(max_done, u + 1)
                pe.wait_ge(a_free, u * NCH + NCH + (0 if last else TURN - BANKS + 1))
                pe.transpose(ps[0:HG * T, PS_A + bank((g + 1) % NG, TURN), 0:P],
                             mx[:, g % 2].rearrange("p h t -> p (h t)"), ident[:, :]).then_inc(turned, 1)

            def scores_for_exp(un, i, h):
                b, g, u = un
                n = i * HG + h
                if n == 0:
                    pe.wait_ge(m_in[g], b * DMA + DMA)
                reuse(pe, exp_done, earlier(u, g, n, NEXP))
                for j, at, q0, w in PIECES[i][1]:
                    ins = pe.matmul(ps[:, PS_B + bank(g, n), at:at + w], k[0:AUG, g, h, j * P:(j + 1) * P],
                                    q[0:AUG, g, h, q0:q0 + w], start=True, stop=True)
                ins.then_inc(b_ready, 1)

            def weigh(un, i, part):
                b, g, u = un
                c, blocks = PIECES[i]
                if part == 0:
                    if i == 0:
                        pe.wait_ge(v_in[g], b * DMA + DMA)
                        reuse(pe, o_copied, u * 2 - 1)
                    if i == HALF0:
                        reuse(pe, o_copied, u * 2)
                    pe.wait_ge(exp_done, u * NEXP + (i + 1) * HG)
                    if diag(PIECES[i]):
                        pe.wait_ge(sel_done, u * NSEL + cut(PIECES[:i + 1]))
                if len(blocks) == 2:
                    todo = [blocks[0][:1] + blocks[0][1:3] + (256,)] if part == 0 else \
                        [(blocks[0][0], 256, blocks[0][2] + 256, 128), blocks[1]]
                else:
                    j, at, q0, w = blocks[0]
                    todo = [(j, at + part * w // 2, q0 + part * w // 2, w // 2)]
                for j, at, q0, w in todo:
                    for h in range(HG):
                        col = q0 - c * HALF
                        ins = pe.matmul(ps[32 * h:32 * h + 32, PS_O + c, col:col + w], v[:, g, j, h, :],
                                        prob[:, (g * NPC + i) % RING, h, at:at + w],
                                        start=(i in (0, HALF0) and part == 0),
                                        stop=(i in (HALF0 - 1, NPC - 1)), skip_group_check=True)
                if part == 1:
                    ins.then_inc(pv_done, 1)

            def prologue():
                for n in range(AHEAD):
                    for c in range(NCH):
                        if c == TURN and n:
                            turn_max(unit(0, n - 1))
                        scores_for_max(unit(0, n), c)
                pe.wait_ge(ones_set, NG)

            def before(un):
                b, g, u = un
                return (b, g - 1, u - 1) if g else (b - 1, NG - 1, u - 1)

            def step(un, ahead, first=False):
                b, g, u = un
                for i in range(NPC):
                    for h in range(HG):
                        scores_for_exp(un, i, h)
                        for c in WITH[i * HG + h] if ahead is not None else ():
                            if c == TURN:
                                turn_max(before(ahead))
                            scores_for_max(ahead, c)
                        if ahead is None and g == NG - AHEAD and (i, h) == (1, 0):
                            turn_max(unit(LAST, NG - 1), last=True)
                        if h % 2 and i >= LAG:
                            weigh(un, i - LAG, h // 2)
                        elif h % 2 and not first:
                            weigh(before(un), NPC + i - LAG, h // 2)

            prologue()
            for n in range(NG):
                step(unit(0, n), unit(0, n + AHEAD), first=(n == 0))
            with pe.Fori(1, LAST) as b:
                for n in range(NG):
                    step(unit(b, n), unit(b, n + AHEAD))
            for n in range(NG):
                step(unit(LAST, n), unit(LAST, n + AHEAD) if n + AHEAD < NG else None)
            for i in range(NPC - LAG, NPC):
                for part in range(2):
                    weigh(unit(LAST, NG - 1), i, part)


def phase3(nc, B, L, D, ps, ident, wo, ones3, mods_d, out_bias_d, resid_d, att_d, out):
    T = L // P
    KC = D // P
    DH = D // HEADS
    PS_A, PS_T, PS_C = 0, 2, 4
    with ExitStack() as ctx:
        sb = lambda n, s, d: ctx.enter_context(nc.sbuf_tensor(n, s, d))
        sem = lambda n: ctx.enter_context(nc.semaphore(n))
        pair = lambda n: (sem(n + "0"), sem(n + "1"))
        att = sb("att_b", [P, 2, NG, L], F32)
        res = sb("res_b", [P, 2, T, D], F32)
        gate = sb("gate_b", [P, 2, D], F32)
        ob = sb("ob_b", [3, 2, D], BF16)
        wg = sb("wg", [P, 2, KC, D], F32)
        rec = sb("rec", [P, 2, HEADS], F32)
        norm = sb("norm", [P, 2, D], F32)
        n_t = sb("n_t", [P, 2, KC, P], F32)
        x2 = sb("x2", [P, 2, T, D], F32)
        att_in, small_in, res_in = pair("p3_att_in"), pair("p3_small_in"), pair("p3_res_in")
        wg_done = sem("p3_wg")
        at_done, rec_done, norm_done = sem("p3_at"), sem("p3_rec"), sem("p3_norm")
        nt_done, nt_copied = sem("p3_nt"), sem("p3_nt_copied")
        c_done, x2_done = sem("p3_c"), sem("p3_x2")
        stored = pair("p3_stored")
        block = ctx.enter_context(nc.Block())

        def loop(eng, work):
            for p in range(2):
                work(p, 0, p)
            with eng.Fori(1, B // 2) as it:
                for p in range(2):
                    work(it * 2 + p, it, p)

        def load(sp, b, p):
            sp.dma_start(att[:, p], att_d[b].rearrange("g p t -> p g t")).then_inc(att_in[p], DMA)
            sp.dma_start(res[:, p], resid_d[b]).then_inc(res_in[p], DMA)
            sp.dma_start(gate[:, p], mods_d[b, M_GA, :].partition_broadcast(P)).then_inc(small_in[p], DMA)
            sp.dma_start(ob[:, p], out_bias_d[b]).then_inc(small_in[p], DMA)

        @block.sync
        def _(sp):
            def store(b, p):
                sp.wait_ge(x2_done, b * T + T)
                sp.dma_start(out[b].rearrange("(t p) d -> p t d", p=P), x2[:, p]).then_inc(stored[p], DMA)

            load(sp, 0, 0)
            load(sp, 1, 1)
            for p in range(2):
                store(p, p)
                load(sp, p + 2, p)
            with sp.Fori(1, B // 2 - 1) as it:
                for p in range(2):
                    store(it * 2 + p, p)
                    load(sp, it * 2 + p + 2, p)
            for p in range(2):
                store(B - 2 + p, p)
            for p in range(2):
                sp.wait_ge(stored[p], DMA * (B // 2))

        @block.vector
        def _(dve):
            def work(b, half, p):
                dve.wait_ge(small_in[p], half * (2 * DMA) + 2 * DMA)
                reuse(dve, stored[p], half * DMA)
                for k in range(KC):
                    ins = dve.tensor_tensor(wg[:, p, k, :], wo[:, k, :], gate[:, p, :], ALU.mult)
                ins.then_inc(wg_done, 1)
                dve.wait_ge(res_in[p], half * DMA + DMA)
                for t in range(T + 2):
                    if t < T:
                        s = t % 2
                        dve.wait_ge(at_done, b * T + t + 1)
                        heads = ps[:, PS_A + s, :].rearrange("p (h n) -> p h n", h=HEADS)
                        dve.reciprocal(rec[:, s, :].rearrange("p (h o) -> p h o", o=1), heads[:, :, DH:DH + 1]) \
                           .then_inc(rec_done, 1)
                        dve.wait_ge(rec_done, b * T + t + 1)
                        reuse(dve, nt_done, b * T + t - 1)
                        dve.tensor_tensor(norm[:, s, :].rearrange("p (h n) -> p h n", h=HEADS), heads[:, :, 0:DH],
                                          rec[:, s, :].rearrange("p (h o) -> p h o", o=1).to_broadcast([P, HEADS, DH]),
                                          ALU.mult).then_inc(norm_done, 1)
                    if t >= 2:
                        s = t % 2
                        dve.wait_ge(c_done, b * T + t - 1)
                        dve.tensor_tensor(x2[:, p, t - 2, :], ps[:, PS_C + s, 0:D], res[:, p, t - 2, :], ALU.add) \
                           .then_inc(x2_done, 1)

            loop(dve, work)

        @block.scalar
        def _(act):
            def work(b, half, p):
                for t in range(T):
                    act.wait_ge(nt_done, b * T + t + 1)
                    reuse(act, c_done, b * T + t - 1)
                    nc.scalar.copy(n_t[:, t % 2], ps[:, PS_T + t % 2, 0:D].rearrange("p (k n) -> p k n", k=KC)) \
                      .then_inc(nt_copied, 1)

            loop(act, work)

        @block.tensor
        def _(pe):
            def work(b, half, p):
                pe.wait_ge(att_in[p], half * DMA + DMA)
                for t in range(T + 2):
                    s = t % 2
                    if t < T:
                        reuse(pe, norm_done, b * T + t - 1)
                        for g in range(NG):
                            ins = pe.transpose(ps[:, PS_A + s, g * P:(g + 1) * P], att[:, p, g, t * P:(t + 1) * P],
                                               ident[:, :])
                        ins.then_inc(at_done, 1)
                    if 1 <= t <= T:
                        r = t - 1
                        pe.wait_ge(norm_done, b * T + r + 1)
                        reuse(pe, nt_copied, b * T + r - 1)
                        for k in range(KC):
                            ins = pe.transpose(ps[:, PS_T + r % 2, k * P:(k + 1) * P],
                                               norm[:, r % 2, k * P:(k + 1) * P], ident[:, :])
                        ins.then_inc(nt_done, 1)
                    if t >= 2:
                        r = t - 2
                        if r == 0:
                            pe.wait_ge(wg_done, b + 1)
                        pe.wait_ge(nt_copied, b * T + r + 1)
                        reuse(pe, x2_done, b * T + r - 1)
                        o = ps[:, PS_C + r % 2, 0:D]
                        pe.matmul(o, ones3[:, :], ob[:, p, :], start=True, stop=False)
                        for k in range(KC):
                            ins = pe.matmul(o, n_t[:, r % 2, k, :], wg[:, p, k, :], start=False, stop=(k == KC - 1))
                        ins.then_inc(c_done, 1)

            loop(pe, work)


def phase4(nc, a, SB, ps, ident, ones3, mods_d, b2_d, tok_d, out):
    SEL, W = tok_d.shape
    D = mods_d.shape[2]
    E = W - D
    C = a["L0_ffn_top_idx"].shape[0]
    FF = a["L0_ffn_W1"].shape[2]
    KC, CT, FT, NT = D // P, C // P, FF // P, SEL // P
    PER_B = NT // SB
    PS_X, PS_H, PS_Y, PS_S = 0, 2, 4, 6
    with ExitStack() as ctx:
        sb = lambda n, s, d: ctx.enter_context(nc.sbuf_tensor(n, s, d))
        sem = lambda n: ctx.enter_context(nc.semaphore(n))
        pair = lambda n: (sem(n + "0"), sem(n + "1"))
        x2 = sb("x2_all", [P, NT, D], F32)
        h2 = sb("h2", [P, NT, D], F32)
        mods = sb("mods_4", [P, SB, 3, D], F32)
        st = sb("st4", [P, NT, 6], F32)
        ag = sb("ag4", [P, NT, 2], F32)
        eps = sb("eps4", [P, 1], F32)
        sd = sb("sd4", [P, NT], F32)
        rs = sb("rs4", [P, NT], F32)
        idx = sb("idx", [P, CT, E], I32)
        idxf = sb("idxf", [P, E, CT], F32)
        iota = sb("iota", [P, SEL], F32)
        b1r = sb("b1r", [E * FT, P], F32)
        b1 = sb("b1", [P, E * FT], F32)
        b2 = sb("b2", [3, E * D], BF16)
        w1 = sb("w1", [P, 2, KC, FF], F32)
        w2 = sb("w2", [P, 2, FT, D], F32)
        gx = sb("gx", [P, 2, CT, W], F32)
        gx_t = sb("gx_t", [P, KC, C], F32)
        hid = sb("hid", [P, FT, C], F32)
        y = sb("y", [P, E * CT, D], F32)
        hot = sb("hot", [P, 2, E * CT, P], F32)
        gated = sb("gated", [P, 2, D], F32)
        x3 = sb("x3", [P, 2, D], F32)

        loaded, x_in = sem("p4_loaded"), sem("p4_x_in")
        w_in = pair("p4_w_in")
        chain = sem("p4_chain")
        ag_done, sd_done, rs_done = sem("p4_ag"), sem("p4_sd"), sem("p4_rs")
        xn_done, h_mul, v_mul, h_done, h_stored = sem("p4_xn"), sem("p4_h_mul"), sem("p4_v_mul"), sem("p4_h"), sem("p4_h_stored")
        g_in = pair("p4_g_in")
        b1_done, b1_copied = sem("p4_b1"), sem("p4_b1_copied")
        gt_done, gt_copied = sem("p4_gt"), sem("p4_gt_copied")
        hid_done, act_done = sem("p4_hid"), sem("p4_act")
        y_done, y_scaled = sem("p4_y"), sem("p4_y_scaled")
        hot_done, s_done, s_gated, s_added = sem("p4_hot"), sem("p4_s"), sem("p4_s_gated"), sem("p4_s_added")
        stored = pair("p4_stored")
        block = ctx.enter_context(nc.Block())
        NLOAD = 4 + SB
        BY_DVE = 2 * NT // 3

        @block.sync
        def _(sp):
            sp.dma_start(x2[:, :, :], out[0:SB].rearrange("b (t p) d -> p (b t) d", p=P)).then_inc(x_in, DMA)
            for b in range(SB):
                sp.dma_start(mods[:, b], mods_d[b, M_SB:M_GB + 1, :].partition_broadcast(P)) \
                  .then_inc(loaded, DMA)
            with nc.allow_non_contiguous_dma("a few indices per row"):
                sp.dma_start(idx[:, :, :], a["L0_ffn_top_idx"].rearrange("(c p) e -> p c e", p=P)).then_inc(loaded, DMA)
            sp.dma_start(iota[:, :], a["const_iota"].partition_broadcast(P)).then_inc(loaded, DMA)
            sp.dma_start(b1r[:, :], a["L0_ffn_b1"].rearrange("e (f p) -> (e f) p", p=P)).then_inc(loaded, DMA)
            sp.dma_start(b2[:, :], b2_d).then_inc(loaded, DMA)

            def weights(e):
                if e >= 2:
                    sp.wait_ge(y_done, (e - 1) * CT)
                sp.dma_start(w1[:, e % 2], a["L0_ffn_W1"][e].rearrange("(k p) f -> p k f", p=P)).then_inc(w_in[e % 2], DMA)
                sp.dma_start(w2[:, e % 2], a["L0_ffn_W2"][e].rearrange("(f p) d -> p f d", p=P)).then_inc(w_in[e % 2], DMA)

            for e in range(2):
                weights(e)
            sp.wait_ge(h_done, NT)
            sp.dma_start(tok_d[:, 0:D].rearrange("(n p) d -> p n d", p=P), h2[:, :, :]).then_inc(h_stored, DMA)
            for e in range(2, E):
                weights(e)
            for n in range(NT):
                b, t = n // PER_B, n % PER_B
                sp.wait_ge(s_added, n + 1)
                sp.dma_start(out[b, t * P:(t + 1) * P, :], x3[:, n % 2, :]).then_inc(stored[n % 2], DMA)
            for p in range(2):
                sp.wait_ge(stored[p], DMA * (NT // 2))

        @block.gpsimd
        def _(pool):
            pool.wait_ge(loaded, DMA * NLOAD)
            for i, n in enumerate(range(BY_DVE, NT)):
                b = n // PER_B
                pool.wait_ge(xn_done, i + 1)
                pool.tensor_tensor(h2[:, n, :], h2[:, n, :], mods[:, b, 1, :], ALU.mult).then_inc(h_mul, 1)
                pool.wait_ge(h_mul, i + 1)
                pool.tensor_tensor(h2[:, n, :], h2[:, n, :], mods[:, b, 0, :], ALU.add).then_inc(h_done, 1)
            pool.wait_ge(h_stored, DMA)
            for e in range(E):
                if e >= 2:
                    pool.wait_ge(y_scaled, (e - 1) * CT)
                for c in range(CT):
                    pool.indirect_dma_start(
                        gx[:, e % 2, c, :], None, tok_d,
                        bass.IndirectOffsetOnAxis(ap=idx[:, c, e:e + 1].bitcast(U32), axis=0)).then_inc(g_in[e % 2], DMA)

        @block.vector
        def _(dve):
            dve.memset(eps[:, :], EPS)
            dve.wait_ge(x_in, DMA)
            for n in range(NT):
                ins = dve.bn_stats(st[:, n, :], x2[:, n, :])
            ins.then_inc(chain, 1)
            dve.wait_ge(chain, 1)
            for n in range(NT):
                ins = dve.bn_aggr(ag[:, n, :], st[:, n, :])
            ins.then_inc(ag_done, 1)
            dve.wait_ge(sd_done, 1)
            dve.reciprocal(rs[:, :], sd[:, :]).then_inc(rs_done, 1)
            dve.wait_ge(rs_done, 1)
            for n in [*range(BY_DVE, NT), *range(BY_DVE)]:
                dve.tensor_scalar(h2[:, n, :], x2[:, n, :], ag[:, n, 0:1], rs[:, n:n + 1], ALU.subtract, ALU.mult) \
                   .then_inc(xn_done, 1)
            dve.wait_ge(loaded, DMA * NLOAD)
            for n in range(BY_DVE):
                dve.wait_ge(xn_done, NT - BY_DVE + n + 1)
                dve.tensor_tensor(h2[:, n, :], h2[:, n, :], mods[:, n // PER_B, 1, :], ALU.mult).then_inc(v_mul, 1)
            for n in range(BY_DVE):
                dve.wait_ge(v_mul, n + 1)
                dve.tensor_tensor(h2[:, n, :], h2[:, n, :], mods[:, n // PER_B, 0, :], ALU.add).then_inc(h_done, 1)
            dve.tensor_copy(idxf[:, :, :], idx[:, :, :].rearrange("p c e -> p e c")).then_inc(chain, 1)
            dve.wait_ge(b1_done, 1)
            dve.tensor_copy(b1[:, :], ps[:, PS_S, 0:E * FT]).then_inc(b1_copied, 1)
            dve.wait_ge(chain, 2)

            def one_hot(n):
                if n >= 2:
                    dve.wait_ge(s_done, n - 1)
                ids = idxf[:, :, :].rearrange("p e (c o) -> p (e c) o", o=1).to_broadcast([P, E * CT, P])
                toks = iota[:, n * P:(n + 1) * P].rearrange("p (o n) -> p o n", o=1).to_broadcast([P, E * CT, P])
                dve.tensor_tensor(hot[:, n % 2], toks, ids, ALU.is_equal).then_inc(hot_done, 1)

            for e in range(E):
                for c in range(CT):
                    dve.wait_ge(gt_done, e * CT + c + 1)
                    if c == 0 and e >= 1:
                        dve.wait_ge(hid_done, e * FT)
                    dve.tensor_copy(gx_t[:, :, c * P:(c + 1) * P],
                                    ps[:, PS_X + c % 2, 0:D].rearrange("p (k n) -> p k n", k=KC)).then_inc(gt_copied, 1)
                for c in range(CT):
                    n = e * CT + c
                    dve.wait_ge(y_done, n + 1)
                    dve.tensor_scalar(y[:, n, :], ps[:, PS_Y + c % 2, 0:D], gx[:, e % 2, c, D + e:D + e + 1], None,
                                      ALU.mult).then_inc(y_scaled, 1)
                if e >= E - 2:
                    one_hot(e - (E - 2))
            for n in range(NT):
                b = n // PER_B
                dve.wait_ge(s_done, n + 1)
                dve.tensor_tensor(gated[:, n % 2, :], ps[:, PS_S + n % 2, 0:D], mods[:, b, 2, :], ALU.mult) \
                   .then_inc(s_gated, 1)
                if n + 2 < NT:
                    one_hot(n + 2)
                dve.wait_ge(s_gated, n + 1)
                if n >= 2:
                    dve.wait_ge(stored[n % 2], DMA * (n // 2))
                dve.tensor_tensor(x3[:, n % 2, :], gated[:, n % 2, :], x2[:, n, :], ALU.add).then_inc(s_added, 1)

        @block.scalar
        def _(act):
            act.wait_ge(ag_done, 1)
            nc.scalar.activation(sd[:, :], ag[:, :, 1], ACT.Sqrt, bias=eps[:, :]).then_inc(sd_done, 1)
            act.wait_ge(b1_copied, 1)
            for e in range(E):
                for f in range(FT):
                    n = e * FT + f
                    act.wait_ge(hid_done, n + 1)
                    if f == 0 and e >= 1:
                        act.wait_ge(y_done, e * CT)
                    nc.scalar.activation(hid[:, f, :], ps[:, PS_H + f % 2, :], ACT.Gelu_apprx_tanh,
                                         bias=b1[:, n:n + 1]).then_inc(act_done, 1)

        @block.tensor
        def _(pe):
            pe.wait_ge(loaded, DMA * NLOAD)
            pe.transpose(ps[:, PS_S, 0:E * FT], b1r[:, :], ident[0:E * FT, 0:E * FT]).then_inc(b1_done, 1)

            def turn(e):
                pe.wait_ge(g_in[e % 2], DMA * CT * (e // 2 + 1))
                for c in range(CT):
                    n = e * CT + c
                    if n >= 2:
                        pe.wait_ge(gt_copied, n - 1)
                    for k in range(KC):
                        ins = pe.transpose(ps[:, PS_X + c % 2, k * P:(k + 1) * P], gx[:, e % 2, c, k * P:(k + 1) * P],
                                           ident[:, :])
                    ins.then_inc(gt_done, 1)

            for e in range(E):
                turn(e)
                pe.wait_ge(w_in[e % 2], 2 * DMA * (e // 2 + 1))
                pe.wait_ge(gt_copied, (e + 1) * CT)
                for f in range(FT):
                    n = e * FT + f
                    if n >= 2:
                        pe.wait_ge(act_done, n - 1)
                    for k in range(KC):
                        ins = pe.matmul(ps[:, PS_H + f % 2, :], w1[:, e % 2, k, f * P:(f + 1) * P], gx_t[:, k, :],
                                        start=(k == 0), stop=(k == KC - 1))
                    ins.then_inc(hid_done, 1)
                pe.wait_ge(act_done, (e + 1) * FT)
                for c in range(CT):
                    n = e * CT + c
                    if n >= 2:
                        pe.wait_ge(y_scaled, n - 1)
                    o = ps[:, PS_Y + c % 2, 0:D]
                    pe.matmul(o, ones3[:, :], b2[:, e * D:(e + 1) * D], start=True, stop=False)
                    for f in range(FT):
                        ins = pe.matmul(o, hid[:, f, c * P:(c + 1) * P], w2[:, e % 2, f, :], start=False,
                                        stop=(f == FT - 1))
                    ins.then_inc(y_done, 1)
            pe.wait_ge(b1_copied, 1)
            pe.wait_ge(y_scaled, E * CT)
            for n in range(NT):
                pe.wait_ge(hot_done, n + 1)
                if n >= 2:
                    pe.wait_ge(s_gated, n - 1)
                for r in range(E * CT):
                    ins = pe.matmul(ps[:, PS_S + n % 2, 0:D], hot[:, n % 2, r, :], y[:, r, :], start=(r == 0),
                                    stop=(r == E * CT - 1))
                ins.then_inc(s_done, 1)


_INS = ['L0_attn_x', 'L0_attn_ln_gamma', 'L0_attn_ln_beta', 'L0_attn_Wq', 'L0_attn_bq', 'L0_attn_Wk', 'L0_attn_bk',
        'L0_attn_Wv', 'L0_attn_bv', 'L0_attn_Wo', 'L0_attn_bo', 'L0_ffn_combine_weights', 'L0_ffn_top_idx',
        'L0_ffn_W1', 'L0_ffn_b1', 'L0_ffn_W2', 'L0_ffn_b2', 'L0_c', 'L0_wmod']


def constants(L, DH, SEL):
    f = np.float32
    rel = np.arange(512)[None, :] - 384 - np.arange(P)[:, None]
    freq = (f(1.0) / f(10000.0) ** (np.arange(0, DH, 2, dtype=f) / f(DH))).astype(f)
    ang = np.arange(L, dtype=f)[:, None] * freq[None, :]
    cos, sin = np.cos(ang).astype(f), np.sin(ang).astype(f)
    table = np.concatenate([np.stack([cos, cos], -1).reshape(L, DH), np.stack([sin, -sin], -1).reshape(L, DH)], 1)
    return {
        "const_ident": np.eye(P, dtype=f),
        "const_mask": np.where(rel > 0, f(MASKED), f(0)).astype(f),
        "const_rope": np.ascontiguousarray(table, dtype=f),
        "const_iota": np.arange(SEL, dtype=f),
    }


def kernel(**inputs):
    import numpy as _np
    import concourse.bacc as _bacc
    from concourse import mybir as _mybir
    from concourse.bass_utils import run_bass_kernel_spmd as _run

    nc = _bacc.Bacc("TRN2", target_bir_lowering=False, num_devices=1)
    arrays, aps = {}, {}
    for name in _INS:
        arrays[name] = _np.ascontiguousarray(inputs[name])
    B, L, D = arrays['L0_attn_x'].shape
    arrays.update(constants(L, D // HEADS, arrays['L0_ffn_combine_weights'].shape[0]))
    for name, arr in arrays.items():
        aps[name] = nc.dram_tensor(f"in_{name}", arr.shape, _mybir.dt.from_np(arr.dtype), kind="ExternalInput").ap()
    out = nc.dram_tensor("out_0", (B, L, D), _mybir.dt.from_np(_np.dtype("float32")), kind="ExternalOutput").ap()
    build(nc, aps, out)
    r = _run(nc, [{f"in_{n}": v for n, v in arrays.items()}], core_ids=[0])
    return r.results[0]["out_0"]
```
